# Optimizing a Trainium2 kernel written in Bass

```python
import numpy as np
import jax
import jax.numpy as jnp

def _softmax(x, axis=-1):
    return jax.nn.softmax(x, axis=axis)

def _gelu(x):
    return jax.nn.gelu(x, approximate=True)

def _silu(x):
    return jax.nn.silu(x)

def _sigmoid(x):
    return jax.nn.sigmoid(x)

def _layernorm(x, axis=-1, eps=1e-05):
    m = jnp.mean(x, axis=axis, keepdims=True)
    v = jnp.var(x, axis=axis, keepdims=True)
    return (x - m) / jnp.sqrt(v + eps)

def _scatter_add(tgt, idx, src, axis=0):
    return tgt.at[idx].add(src)

def _segment_sum(src, seg, n):
    return jax.ops.segment_sum(src, seg, n)
kernel_name = 'mk_adaln_d1_jaxref_r8_1dbc68'

def setup_inputs(seed: int=0):
    np.random.seed(seed)
    _w = jnp.asarray

    def _L0_attn_setup():
        import jax, jax.numpy as jnp
        import numpy as np
        D_MODEL = 128
        NUM_HEADS = 16
        HEAD_DIM = D_MODEL // NUM_HEADS
        WINDOW_SIZE = 64
        SCALE = float(np.sqrt(HEAD_DIM))
        key = jax.random.key(seed)
        k1, k2, k3 = jax.random.split(key, 3)
        B, S = (4, 256)
        x = jax.random.normal(k1, (B, S, D_MODEL), dtype=jnp.float32)
        W_qkv = jax.random.normal(k2, (3 * D_MODEL, D_MODEL), dtype=jnp.float32) * (1.0 / np.sqrt(D_MODEL))
        W_o = jax.random.normal(k3, (D_MODEL, D_MODEL), dtype=jnp.float32) * (1.0 / np.sqrt(D_MODEL))
        return {'x': x, 'W_qkv': W_qkv, 'W_o': W_o}
    _L0_attn_in = _L0_attn_setup()

    def _L0_ffn_setup():
        import jax, jax.numpy as jnp
        import numpy as np
        H = 128
        I = 64
        E = 8
        TOPK = 2
        NGROUP = 4
        TOPKG = 2
        SCALE = 1.0
        B, S = (4, 128)

        def _gate(xf, gate_weight, bias):
            T = xf.shape[0]
            logits = xf @ gate_weight.T
            scores = jax.nn.sigmoid(logits)
            scores_for_choice = scores + bias[None, :]
            gsz = E // NGROUP
            grp = scores_for_choice.reshape(T, NGROUP, gsz)
            group_scores = jax.lax.top_k(grp, 2)[0].sum(-1)
            _, group_idx = jax.lax.top_k(group_scores, TOPKG)
            rows = jnp.arange(T)[:, None]
            group_mask = jnp.zeros((T, NGROUP), xf.dtype).at[rows, group_idx].set(1.0)
            score_mask = jnp.broadcast_to(group_mask[:, :, None], (T, NGROUP, gsz)).reshape(T, E)
            tmp_scores = jnp.where(score_mask > 0, scores_for_choice, 0.0)
            _, topk_idx = jax.lax.top_k(tmp_scores, TOPK)
            topk_weight = jnp.take_along_axis(scores, topk_idx, axis=1)
            if TOPK > 1:
                topk_weight = topk_weight / (topk_weight.sum(-1, keepdims=True) + 1e-20)
            topk_weight = topk_weight * SCALE
            return (topk_idx, topk_weight)
        key = jax.random.key(seed)
        k0, k1, k2, k3, k4 = jax.random.split(key, 5)
        return {'hidden_states': jax.random.normal(k0, (B, S, H), jnp.float32), 'gate_weight': jax.random.normal(k1, (E, H), jnp.float32) * (1.0 / np.sqrt(H)), 'e_score_correction_bias': jnp.zeros((E,), jnp.float32), 'gate_proj': jax.random.normal(k2, (E, I, H), jnp.float32) * 0.02, 'up_proj': jax.random.normal(k3, (E, I, H), jnp.float32) * 0.02, 'down_proj': jax.random.normal(k4, (E, H, I), jnp.float32) * 0.02}
    _L0_ffn_in = _L0_ffn_setup()
    _L0_c = _w((lambda *s: np.random.randn(*s).astype(np.float32) * 0.05)(8, 128))
    _L0_wmod = _w((lambda *s: np.random.randn(*s).astype(np.float32) * 0.05)(128, 6 * 128) * 128 ** (-0.5))
    _d = {'L0_attn_x': _L0_attn_in['x'], 'L0_attn_W_qkv': _L0_attn_in['W_qkv'], 'L0_attn_W_o': _L0_attn_in['W_o'], 'L0_ffn_gate_weight': _L0_ffn_in['gate_weight'], 'L0_ffn_e_score_correction_bias': _L0_ffn_in['e_score_correction_bias'], 'L0_ffn_gate_proj': _L0_ffn_in['gate_proj'], 'L0_ffn_up_proj': _L0_ffn_in['up_proj'], 'L0_ffn_down_proj': _L0_ffn_in['down_proj'], 'L0_c': _L0_c, 'L0_wmod': _L0_wmod}
    _x0 = _d['L0_attn_x']
    _d['L0_attn_x'] = jax.random.normal(jax.random.fold_in(jax.random.key(seed), 1), (8, 256, 128), dtype=_x0.dtype)
    del _x0
    return _d

def reference(L0_attn_x, L0_attn_W_qkv, L0_attn_W_o, L0_ffn_gate_weight, L0_ffn_e_score_correction_bias, L0_ffn_gate_proj, L0_ffn_up_proj, L0_ffn_down_proj, L0_c, L0_wmod):

    def _L0_attn_ref(x, W_qkv, W_o):
        import jax, jax.numpy as jnp
        import numpy as np
        D_MODEL = 128
        NUM_HEADS = 16
        HEAD_DIM = D_MODEL // NUM_HEADS
        WINDOW_SIZE = 64
        SCALE = float(np.sqrt(HEAD_DIM))
        B, S, _ = x.shape
        qkv = jnp.einsum('bsd,ed->bse', x, W_qkv)
        qkv = qkv.reshape(B, S, 3, NUM_HEADS, HEAD_DIM)
        qkv = jnp.transpose(qkv, (2, 0, 3, 1, 4))
        Q, K, V = (qkv[0], qkv[1], qkv[2])
        idx = jnp.arange(S)
        half = WINDOW_SIZE // 2
        mask = jnp.abs(idx[:, None] - idx[None, :]) <= half
        scores = jnp.einsum('bhqd,bhkd->bhqk', Q, K) / SCALE
        scores = jnp.where(mask[None, None], scores, -jnp.inf)
        attn = jax.nn.softmax(scores, axis=-1)
        out = jnp.einsum('bhqk,bhkd->bhqd', attn, V)
        out = jnp.transpose(out, (0, 2, 1, 3)).reshape(B, S, D_MODEL)
        return jnp.einsum('bsd,ed->bse', out, W_o)

    def _L0_ffn_ref(hidden_states, gate_weight, e_score_correction_bias, gate_proj, up_proj, down_proj):
        import jax, jax.numpy as jnp
        import numpy as np
        H = 128
        I = 64
        E = 8
        TOPK = 2
        NGROUP = 4
        TOPKG = 2
        SCALE = 1.0
        B, S = (4, 128)

        def _gate(xf, gate_weight, bias):
            T = xf.shape[0]
            logits = xf @ gate_weight.T
            scores = jax.nn.sigmoid(logits)
            scores_for_choice = scores + bias[None, :]
            gsz = E // NGROUP
            grp = scores_for_choice.reshape(T, NGROUP, gsz)
            group_scores = jax.lax.top_k(grp, 2)[0].sum(-1)
            _, group_idx = jax.lax.top_k(group_scores, TOPKG)
            rows = jnp.arange(T)[:, None]
            group_mask = jnp.zeros((T, NGROUP), xf.dtype).at[rows, group_idx].set(1.0)
            score_mask = jnp.broadcast_to(group_mask[:, :, None], (T, NGROUP, gsz)).reshape(T, E)
            tmp_scores = jnp.where(score_mask > 0, scores_for_choice, 0.0)
            _, topk_idx = jax.lax.top_k(tmp_scores, TOPK)
            topk_weight = jnp.take_along_axis(scores, topk_idx, axis=1)
            if TOPK > 1:
                topk_weight = topk_weight / (topk_weight.sum(-1, keepdims=True) + 1e-20)
            topk_weight = topk_weight * SCALE
            return (topk_idx, topk_weight)
        Bv, Sv, Hv = hidden_states.shape
        xf = hidden_states.reshape(-1, Hv).astype(jnp.float32)
        topk_idx, topk_weight = _gate(xf, gate_weight.astype(jnp.float32), e_score_correction_bias.astype(jnp.float32))
        y = jnp.zeros_like(xf)
        for e in range(E):
            combine_w = jnp.where(topk_idx == e, topk_weight, 0.0).sum(-1)
            g = xf @ gate_proj[e].T
            u = xf @ up_proj[e].T
            o = jax.nn.silu(g) * u @ down_proj[e].T
            y = y + combine_w[:, None] * o
        return y.reshape(Bv, Sv, Hv)
    x = L0_attn_x
    mod = (_silu(L0_c) @ L0_wmod).reshape(L0_c.shape[0], 6, 1, -1)
    sa, ca, ga, sb, cb, gb = (mod[:, 0], mod[:, 1], mod[:, 2], mod[:, 3], mod[:, 4], mod[:, 5])
    ga = (2 * (ga >= 0) - 1) * jnp.maximum(jnp.abs(ga), 0.25)
    gb = (2 * (gb >= 0) - 1) * jnp.maximum(jnp.abs(gb), 0.25)
    h = _layernorm(x, axis=-1) * (1 + ca) + sa
    x = x + ga * _L0_attn_ref(h, L0_attn_W_qkv, L0_attn_W_o)
    h = _layernorm(x, axis=-1) * (1 + cb) + sb
    x = x + gb * _L0_ffn_ref(h, L0_ffn_gate_weight, L0_ffn_e_score_correction_bias, L0_ffn_gate_proj, L0_ffn_up_proj, L0_ffn_down_proj)
    return x

_drawn_inputs = setup_inputs


def setup_inputs(seed=0):
    import zlib

    import numpy as np

    out = dict(_drawn_inputs(seed))
    spreads = {'L0_ffn_e_score_correction_bias': (0.0, 0.8)}
    factors = {'L0_ffn_gate_weight': 8.0,
     'L0_ffn_gate_proj': 8.0,
     'L0_ffn_up_proj': 8.0,
     'L0_ffn_down_proj': 8.0}
    for name, (base, spread) in spreads.items():
        noise = np.random.default_rng([zlib.crc32(name.encode()), seed]).standard_normal(out[name].shape)
        drawn = base * np.exp(spread * noise) if base else spread * noise
        out[name] = jnp.asarray(drawn.astype(out[name].dtype))
    for name, factor in factors.items():
        out[name] = (out[name] * factor).astype(out[name].dtype)
    return out
```

```python
from contextlib import ExitStack

import numpy as np

import concourse.bass as bass
from concourse import mybir

ALU = mybir.AluOpType
ACT = mybir.ActivationFunctionType
AX = mybir.AxisListType
F32 = mybir.dt.float32
F32R = mybir.dt.float32r
BF16 = mybir.dt.bfloat16

B, S, D = 8, 256, 128
H, DH = 16, 8
HALF = 32
KB = 32
NKB = S // KB
WIN = KB + 2 * HALF
G = D // KB
NHG = H // G
BANKKB = 4
SC = BANKKB * WIN
VW = G * DH + G
E, I = 8, 64
NT = S // 128
EI = E * I
NC_ = EI // 128
NG, GSZ = 4, 2
TOPK = TOPKG = 2
EPS = 1e-5
GATE_MIN = 0.25
MASKED = -1e30
BANK = 512
ROUTE = 4 + 4 + 1 + 4 + 4
MODS = 6
SA, CA, GA, SB, CB, GB = range(MODS)

C_ID = 0
C_MASK = C_ID + 128
C_NI = C_MASK + 2 * KB
C_ONES = C_NI + KB
C_BD = C_ONES + 128
C_DEN = C_BD + G * DH
C_HEAD = C_DEN + G
C_LG = C_HEAD + G
C_LE = C_LG + NG * NG
C_END = C_LE + E * E


USE_LOOP = False


def constants():
    c = np.zeros((128, C_END), np.float32)
    p = np.arange(128)
    g, r = p // KB, p % KB
    c[:, C_ID:C_ID + 128] = np.eye(128)
    q = np.arange(KB)
    c[:, C_MASK:C_MASK + KB] = np.where(r[:, None] <= q[None], 0.0, MASKED)
    c[:, C_MASK + KB:C_MASK + 2 * KB] = np.where(q[None] <= r[:, None], 0.0, MASKED)
    c[:, C_NI:C_NI + KB] = np.where(r[:, None] == q[None], -1.0, 0.0)
    c[:, C_ONES:C_ONES + 128] = g[:, None] == g[None]
    c[:, C_BD:C_BD + G * DH] = g[:, None] == (np.arange(G * DH) // DH)[None]
    c[:, C_DEN:C_DEN + G] = g[:, None] == np.arange(G)[None]
    c[:, C_HEAD:C_HEAD + G] = (p // DH % G)[:, None] == np.arange(G)[None]
    c[:, C_LG:C_LG + NG * NG] = (np.arange(NG)[None] < np.arange(NG)[:, None]).reshape(1, -1)
    c[:, C_LE:C_LE + E * E] = (np.arange(E)[None] < np.arange(E)[:, None]).reshape(1, -1)
    return c


def view(ap, dims):
    return bass.AP(ap.tensor, ap.offset, [list(ap.ap[0])] + [list(d) for d in dims])


def program(nc, x, wq, wk, wv, wo, gate_w, bias, w_gate, w_up, w_down, c_t, wmod, consts, out,
            use_loop=USE_LOOP):
    with ExitStack() as ctx:
        def sb(name, shape, dt=F32):
            return ctx.enter_context(nc.sbuf_tensor(name, shape, dt))

        def sem(name):
            return ctx.enter_context(nc.semaphore(name))

        con = sb("con", [128, C_END])
        wq_sb, wk_sb, wv_sb, wo_sb = (sb(n, [128, D]) for n in ("wq_sb", "wk_sb", "wv_sb", "wo_sb"))
        gw_sb = sb("gw_sb", [128, E])
        bias_sb = sb("bias_sb", [128, NT, E])
        wg_sb, wu_sb = sb("wg_sb", [128, EI]), sb("wu_sb", [128, EI])
        wd_sb = sb("wd_sb", [128, NC_, D])
        ct_sb = sb("ct_sb", [128, B])
        wm_sb = sb("wm_sb", [128, MODS * D])
        ct_t, silu2_c, silu_c = (sb(n, [128, B]) for n in ("ct_t", "silu2_c", "silu_c"))
        mod = sb("mod", [128, MODS, B])
        gsign, gabs, gsize = (sb(n, [128, 2, B]) for n in ("gsign", "gabs", "gsize"))
        gates = sb("gates", [128, 2, B])
        gate_row = sb("gate_row", [128, B, 2, D])
        ident_bf = sb("ident_bf", [128, 128], BF16)
        mask_bf = sb("mask_bf", [128, 2, KB], BF16)
        quad_ones = sb("quad_ones", [128, 128], F32R)
        minus_half = sb("minus_half", [128, NT])

        x_sb = sb("x_sb", [128, NT, D])
        stats1, mv1 = sb("stats1", [128, NT, 6]), sb("mv1", [128, NT, 2])
        veps1, rstd1 = sb("veps1", [128, NT]), sb("rstd1", [128, NT])
        xn1 = sb("xn1", [128, NT, D])
        h_t = sb("h_t", [128, S])
        q_pad = sb("q_pad", [128, HALF + S + HALF])
        k_bd = sb("k_bd", [128, NKB, G, KB])
        h_rep = sb("h_rep", [128, NKB, G, KB])
        v_bd = sb("v_bd", [128, NKB, NHG, VW])

        blkmax = sb("blkmax", [128, 2, 3 * NKB + 2])
        row_max = sb("row_max", [128, NKB])
        shift = sb("shift", [128, 2, HALF + S + HALF], F32R)
        probs = sb("probs", [128, 2, 2 * SC])
        o_t = sb("o_t", [VW, 2, 2 * S])
        rden = sb("rden", [128, NT, H])
        o_n, on_t = sb("o_n", [128, NT, D]), sb("on_t", [128, S])
        wo_g = sb("wo_g", [128, D])
        x_res, x1 = sb("x_res", [128, NT, D]), sb("x1", [128, NT, D])

        stats2, mv2 = sb("stats2", [128, NT, 6]), sb("mv2", [128, NT, 2])
        veps2, rstd2 = sb("veps2", [128, NT]), sb("rstd2", [128, NT])
        xn2 = sb("xn2", [128, NT, D])
        h2_t = sb("h2_t", [128, S])
        ex = sb("ex", [128, NT, E])
        exp1, score, choice = (sb(n, [128, NT, E]) for n in ("exp1", "score", "choice"))
        gsum, grank = sb("gsum", [128, NT, NG]), sb("grank", [128, NT, NG])
        ggt, geq, gtie, gall = (sb(n, [128, NT, NG, NG]) for n in ("ggt", "geq", "gtie", "gall"))
        tmp, rank, wsel, cw = (sb(n, [128, NT, E]) for n in ("tmp", "rank", "wsel", "cw"))
        egt, eeq, etie, eall = (sb(n, [128, NT, E, E]) for n in ("egt", "eeq", "etie", "eall"))
        wsum, wsum2, rsum = (sb(n, [128, NT]) for n in ("wsum", "wsum2", "rsum"))
        tanh_g, gate_a = sb("tanh_g", [128, EI]), sb("gate_a", [128, EI])
        act, act_w = sb("act", [128, NT, EI]), sb("act_w", [128, NT, EI])
        act_t = sb("act_t", [128, NT, NC_, 128])
        y_g, out_sb = sb("y_g", [128, NT, D]), sb("out_sb", [128, NT, D])

        ps = ctx.enter_context(nc.psum_tensor("ps", [128, 8, BANK], F32))
        OB, W0, W1 = 4, 6, 7

        w_loaded, consts_loaded, mod_loaded = sem("w_loaded"), sem("consts_loaded"), sem("mod_loaded")
        zeroed, silu_step, mod_step, consts_made = sem("zeroed"), sem("silu_step"), sem("mod_step"), sem("consts_made")
        dens_made, rank_gt = sem("dens_made"), sem("rank_gt")
        tanh_c_ready, mod_ps, gate_ps, gate_row_ready = (
            sem("tanh_c_ready"), sem("mod_ps"), sem("gate_ps"), sem("gate_row_ready"))
        x_loaded, out_stored = sem("x_loaded"), sem("out_stored")
        xt_ps, qk_ps, v_ps = sem("xt_ps"), sem("qk_ps"), sem("v_ps")
        scores_ps, shifted_ps, pv_ps = sem("scores_ps"), sem("shifted_ps"), sem("pv_ps")
        ot_ps, ont_ps, wo_ps = sem("ot_ps"), sem("ont_ps"), sem("wo_ps")
        h2t_ps, logits_ps, up_ps, actt_ps, down_ps = (
            sem("h2t_ps"), sem("logits_ps"), sem("up_ps"), sem("actt_ps"), sem("down_ps"))
        ln1_stat, ln1_var, xn1_ready, v_ready = sem("ln1_stat"), sem("ln1_var"), sem("xn1_ready"), sem("v_ready")
        max_step, shift_ready = sem("max_step"), sem("shift_ready")
        rden_ready, on_ready, x1_ready, ln2_stat, ln2_var, xn2_ready = (
            sem("rden_ready"), sem("on_ready"), sem("x1_ready"), sem("ln2_stat"), sem("ln2_var"), sem("xn2_ready"))
        route_step, cw_ready, gate_a_ready, act_ready, yg_ready = (
            sem("route_step"), sem("cw_ready"), sem("gate_a_ready"), sem("act_ready"), sem("yg_ready"))
        h_ready, q_ready, k_ready, probs_ready, o_ready, ont_ready = (
            sem("h_ready"), sem("q_ready"), sem("k_ready"), sem("probs_ready"), sem("o_ready"), sem("ont_ready"))
        h2_ready, ex_ready, tanh_ready, actt_ready = (
            sem("h2_ready"), sem("ex_ready"), sem("tanh_ready"), sem("actt_ready"))
        eps1_step, rstd1_ready, eps2_step, rstd2_ready = (
            sem("eps1_step"), sem("rstd1_ready"), sem("eps2_step"), sem("rstd2_ready"))
        hrep_ready, xres_ready, wog_ready, actw_ready, out_ready = (
            sem("hrep_ready"), sem("xres_ready"), sem("wog_ready"), sem("actw_ready"), sem("out_ready"))

        def wait(eng, s, b, per, k):
            v = b * per + k
            if isinstance(v, int) and v <= 0:
                return
            eng.wait_ge(s, v)

        def steps(eng, step):
            step(0, True, True, False)
            if use_loop:
                with eng.Fori(1, B - 1) as i:
                    step(i, True, True, True)
            else:
                for i in range(1, B - 1):
                    step(i, True, True, True)
            step(B - 1, False, True, True)
            step(B, False, False, True)

        ident = con[:, C_ID:C_ID + 128]
        block = ctx.enter_context(nc.Block())

        @block.sync
        def _(sp):
            def load_x(b):
                return sp.dma_start(x_sb[:], x[bass.ds(b, 1)].rearrange("a (t p) d -> p (a t) d", p=128))\
                         .then_inc(x_loaded, 16)

            def step(i, pre, att, ffn):
                if pre:
                    wait(sp, xres_ready, i, 1, 1)
                    wait(sp, xn1_ready, i, NT, NT)
                    load_x(i + 1)
                if ffn:
                    wait(sp, out_ready, i - 1, 1, 1)
                    sp.dma_start(out[bass.ds(i - 1, 1)].rearrange("a (t p) d -> p (a t) d", p=128),
                                 out_sb[:]).then_inc(out_stored, 16)

            load_x(0)
            for dst, src in ((con, consts),):
                sp.dma_start(dst[:], src).then_inc(consts_loaded, 16)
            for dst, src in ((wq_sb, wq), (wk_sb, wk), (wv_sb, wv), (wo_sb, wo), (gw_sb, gate_w),
                             (bias_sb, bias), (wg_sb, w_gate), (wu_sb, w_up), (wd_sb, w_down)):
                sp.dma_start(dst[:], src).then_inc(w_loaded, 16)
            steps(sp, step)
            sp.wait_ge(out_stored, 16 * B)

        @block.gpsimd
        def _(pool):
            def norm_scale(b, var, mv, veps, step_done, rs, used, ready):
                wait(pool, var, b, NT, NT)
                nc.gpsimd.tensor_scalar(veps[:], mv[:, :, 1], EPS, None, ALU.add).then_inc(step_done, 1)
                wait(pool, step_done, b, 1, 1)
                wait(pool, used, b, NT, 0)
                nc.gpsimd.tensor_tensor(rs[:], veps[:], minus_half[:], ALU.pow).then_inc(ready, 1)

            def repeat_h(b):
                wait(pool, h_ready, b, 1, 1)
                wait(pool, v_ps, b, 2, 0)
                nc.gpsimd.tensor_copy(h_rep[:], view(h_t[:, 0:1], [[KB, NKB], [0, G], [1, KB]]))\
                  .then_inc(hrep_ready, 1)

            def step(i, pre, att, ffn):
                if att:
                    wait(pool, x_loaded, i, 16, 16)
                    wait(pool, x1_ready, i, 1, 0)
                    nc.gpsimd.tensor_copy(x_res[:], x_sb[:]).then_inc(xres_ready, 1)
                    wait(pool, wo_ps, i, 1, 0)
                    nc.gpsimd.tensor_tensor(
                        wo_g[:], wo_sb[:], gate_row[:, bass.ds(i, 1), 0, :].rearrange("p a d -> p (a d)"),
                        ALU.mult).then_inc(wog_ready, 1)
                if ffn:
                    for t in range(NT):
                        wait(pool, cw_ready, i - 1, 1, 1)
                        wait(pool, act_ready, i - 1, NT, t + 1)
                        wait(pool, actt_ps, i - 1, NT, 0)
                        nc.gpsimd.tensor_tensor(
                            act_w[:, t, :].rearrange("p (e i) -> p e i", e=E),
                            act[:, t, :].rearrange("p (e i) -> p e i", e=E),
                            view(cw[:, t, :], [[1, E], [0, I]]), ALU.mult).then_inc(actw_ready, 1)
                if pre:
                    norm_scale(i + 1, ln1_var, mv1, veps1, eps1_step, rstd1, xn1_ready, rstd1_ready)
                    repeat_h(i + 1)
                if ffn:
                    wait(pool, yg_ready, i - 1, 1, 1)
                    wait(pool, out_stored, i - 1, 16, 0)
                    nc.gpsimd.tensor_tensor(out_sb[:], y_g[:], x1[:], ALU.add).then_inc(out_ready, 1)
                if att:
                    norm_scale(i, ln2_var, mv2, veps2, eps2_step, rstd2, xn2_ready, rstd2_ready)

            nc.gpsimd.memset(minus_half[:], -0.5).then_inc(zeroed, 1)
            nc.gpsimd.memset(q_pad[:], 0.0).then_inc(zeroed, 1)
            nc.gpsimd.memset(v_bd[:], 0.0).then_inc(zeroed, 1)
            pool.wait_ge(zeroed, 3)
            norm_scale(0, ln1_var, mv1, veps1, eps1_step, rstd1, xn1_ready, rstd1_ready)
            repeat_h(0)
            pool.wait_ge(w_loaded, 9 * 16)
            pool.wait_ge(gate_row_ready, 2)
            steps(pool, step)

        @block.scalar
        def _(act_e):
            def project_inputs(b):
                wait(act_e, xt_ps, b, 1, 1)
                wait(act_e, hrep_ready, b, 1, 0)
                nc.scalar.activation(h_t[:], ps[:, W0, 0:S], ACT.Identity,
                                     scale=mod[:, CA, bass.ds(b, 1)],
                                     bias=mod[:, SA, bass.ds(b, 1)]).then_inc(h_ready, 1)
                wait(act_e, qk_ps, b, 1, 1)
                wait(act_e, scores_ps, b, NHG, 0)
                nc.scalar.activation(q_pad[:, HALF:HALF + S], ps[:, W0, 0:S], ACT.Copy).then_inc(q_ready, 1)

            def exponentials(i, hg):
                wait(act_e, shifted_ps, i, NHG, hg + 1)
                wait(act_e, pv_ps, i, NHG, hg - 1)
                half = hg % 2
                nc.scalar.activation(probs[:, half, :].rearrange("p (b c) -> p b c", b=2),
                                     ps[:, 2 * half:2 * half + 2, 0:SC], ACT.Exp,
                                     scale=float(DH) ** -0.5).then_inc(probs_ready, 1)

            def keep_o(i, pair):
                wait(act_e, pv_ps, i, NHG, 2 * pair + 2)
                wait(act_e, ot_ps, i, 1, 0)
                nc.scalar.activation(o_t[:, pair, :], ps[0:VW, OB + pair, :], ACT.Copy).then_inc(o_ready, 1)

            def tanh_gate(b, t):
                wait(act_e, up_ps, b, NT, t + 1)
                wait(act_e, gate_a_ready, b, NT, t)
                nc.scalar.activation(tanh_g[:], ps[:, W0, :], ACT.Tanh, scale=0.5).then_inc(tanh_ready, 1)

            def keep_act_t(b, t):
                wait(act_e, actt_ps, b, NT, t + 1)
                nc.scalar.activation(act_t[:, t].rearrange("p c n -> p (c n)"), ps[:, W0 + t, :],
                                     ACT.Copy).then_inc(actt_ready, 1)

            def step(i, pre, att, ffn):
                if ffn:
                    wait(act_e, h2t_ps, i - 1, 1, 1)
                    nc.scalar.activation(h2_t[:], ps[:, W0, 0:S], ACT.Identity,
                                         scale=mod[:, CB, bass.ds(i - 1, 1)],
                                         bias=mod[:, SB, bass.ds(i - 1, 1)]).then_inc(h2_ready, 1)
                    wait(act_e, logits_ps, i - 1, 1, 1)
                    wait(act_e, route_step, i - 1, ROUTE, 0)
                    nc.scalar.activation(ex[:].rearrange("p t e -> p (t e)"), ps[:, W1, 0:NT * E], ACT.Exp,
                                         scale=-1.0).then_inc(ex_ready, 1)
                if att:
                    exponentials(i, 0)
                if ffn:
                    tanh_gate(i - 1, 0)
                if att:
                    exponentials(i, 1)
                if ffn:
                    tanh_gate(i - 1, 1)
                if att:
                    exponentials(i, 2)
                    keep_o(i, 0)
                if ffn:
                    keep_act_t(i - 1, 0)
                if att:
                    exponentials(i, 3)
                if ffn:
                    keep_act_t(i - 1, 1)
                if pre:
                    project_inputs(i + 1)
                if att:
                    keep_o(i, 1)
                    wait(act_e, ont_ps, i, 1, 1)
                    nc.scalar.activation(on_t[:], ps[:, W1, 0:S], ACT.Copy).then_inc(ont_ready, 1)

            act_e.dma_start(ct_sb[:], c_t).then_inc(mod_loaded, 16)
            act_e.dma_start(wm_sb[:], wmod).then_inc(mod_loaded, 16)
            nc.scalar.preload_act_table(ACT.Exp)
            act_e.wait_ge(mod_loaded, 32)
            nc.scalar.activation(ct_t[:], ct_sb[:], ACT.Tanh, scale=0.5).then_inc(tanh_c_ready, 1)
            act_e.wait_ge(mod_step, 6)
            act_e.wait_ge(zeroed, 3)
            project_inputs(0)
            for half in range(2):
                act_e.wait_ge(gate_ps, 2)
                nc.scalar.activation(gate_row[:, 4 * half:4 * half + 4].rearrange("p b w d -> p (b w d)"),
                                     ps[:, 2 * half:2 * half + 2, :].rearrange("p b c -> p (b c)"),
                                     ACT.Copy).then_inc(gate_row_ready, 1)
            steps(act_e, step)

        @block.tensor
        def _(pe):
            def transpose_norm(b, xn, ready, done):
                wait(pe, ready, b, NT, NT)
                for t in range(NT):
                    last = nc.tensor.transpose(ps[:, W0, t * 128:(t + 1) * 128], xn[:, t, :], ident)
                last.then_inc(done, 1)

            def transpose_x(b):
                wait(pe, v_ready, b, 2, 0)
                wait(pe, actt_ready, b - 2, NT, 1)
                transpose_norm(b, xn1, xn1_ready, xt_ps)

            def project_qk(b):
                wait(pe, h_ready, b, 1, 1)
                nc.tensor.matmul(ps[:, W0, 0:S], wq_sb[:], h_t[:], start=True, stop=True)
                nc.tensor.matmul(ps[:, W0, S:2 * S], wk_sb[:], h_t[:], start=True, stop=True)\
                  .then_inc(qk_ps, 1)

            def project_v(b, half):
                if half == 0:
                    wait(pe, hrep_ready, b, 1, 1)
                    wait(pe, k_ready, b, 1, 1)
                    wait(pe, q_ready, b, 1, 1)
                else:
                    wait(pe, v_ready, b, 2, 1)
                for j in range(BANKKB):
                    kb = half * BANKKB + j
                    last = nc.tensor.matmul(ps[:, W0, j * D:(j + 1) * D],
                                            h_rep[:, kb].rearrange("p g k -> p (g k)"), wv_sb[:],
                                            start=True, stop=True)
                last.then_inc(v_ps, 1)

            def scores(i, hg):
                half = hg % 2
                if hg == 0:
                    wait(pe, k_ready, i, 1, 1)
                    wait(pe, q_ready, i, 1, 1)
                wait(pe, probs_ready, i, NHG, hg - 1)
                rows = slice(G * DH * hg, G * DH * (hg + 1))
                for kb in range(NKB):
                    bank, j = 2 * half + kb // BANKKB, kb % BANKKB
                    nc.tensor.matmul(ps[:, bank, j * WIN:(j + 1) * WIN],
                                     k_bd[rows, kb].rearrange("p g k -> p (g k)"),
                                     q_pad[rows, kb * KB:kb * KB + WIN],
                                     start=(j == 0), stop=False, skip_group_check=True)
                for bank in (2 * half, 2 * half + 1):
                    last = nc.tensor.matmul(
                        view(ps[:, bank, 0:1], [[WIN, BANKKB], [2 * KB, 2], [1, KB]]), ident_bf[:],
                        view(mask_bf[:, 0, 0:1], [[0, BANKKB], [KB, 2], [1, KB]]),
                        start=False, stop=False, skip_group_check=True)
                last.then_inc(scores_ps, 1)

            def subtract_max(i, hg):
                half = hg % 2
                wait(pe, shift_ready, i, NHG, hg + 1)
                for j in range(2):
                    last = nc.tensor.matmul(
                        ps[:, 2 * half + j, 0:SC], quad_ones[:],
                        view(shift[:, half, j * BANKKB * KB:j * BANKKB * KB + 1], [[KB, BANKKB], [1, WIN]]),
                        start=False, stop=True, skip_group_check=True)
                last.then_inc(shifted_ps, 1)

            def weigh_values(i, hg):
                half = hg % 2
                wait(pe, probs_ready, i, NHG, hg + 1)
                if hg == 0:
                    wait(pe, v_ready, i, 2, 2)
                if half == 0:
                    wait(pe, o_ready, i - 1, 2, hg // 2 + 1)
                for kb in range(NKB):
                    lo, hi = max(0, (kb - 1) * KB), min(S, (kb + 2) * KB)
                    at = kb * WIN + lo - (kb - 1) * KB
                    last = nc.tensor.matmul(ps[0:VW, OB + hg // 2, half * S + lo:half * S + hi],
                                            v_bd[:, kb, hg, :], probs[:, half, at:at + hi - lo],
                                            start=(half == 0 and kb == 0), stop=(kb == NKB - 1),
                                            skip_group_check=True)
                last.then_inc(pv_ps, 1)

            def logits(b):
                wait(pe, h2_ready, b, 1, 1)
                wait(pe, x1_ready, b, 1, 1)
                for t in range(NT):
                    last = nc.tensor.matmul(ps[:, W1, t * E:(t + 1) * E], h2_t[:, t * 128:(t + 1) * 128],
                                            gw_sb[:], start=True, stop=True)
                last.then_inc(logits_ps, 1)

            def up(b, t):
                if t == 0:
                    wait(pe, ex_ready, b, 1, 1)
                else:
                    wait(pe, act_ready, b, NT, t)
                h2 = h2_t[:, t * 128:(t + 1) * 128]
                nc.tensor.matmul(ps[:, W0, :], h2, wg_sb[:], start=True, stop=True)
                nc.tensor.matmul(ps[:, W1, :], h2, wu_sb[:], start=True, stop=True).then_inc(up_ps, 1)

            def transpose_act(b, t):
                wait(pe, actw_ready, b, NT, t + 1)
                wait(pe, act_ready, b, NT, NT)
                for c in range(NC_):
                    last = nc.tensor.transpose(ps[:, W0 + t, c * 128:(c + 1) * 128],
                                               act_w[:, t, c * 128:(c + 1) * 128], ident)
                last.then_inc(actt_ps, 1)

            def down(b):
                wait(pe, actt_ready, b, NT, NT)
                for t in range(NT):
                    for c in range(NC_):
                        last = nc.tensor.matmul(ps[:, W1, t * D:(t + 1) * D], act_t[:, t, c, :],
                                                wd_sb[:, c, :], start=(c == 0), stop=(c == NC_ - 1))
                last.then_inc(down_ps, 1)

            def transpose_o(i):
                wait(pe, o_ready, i, 2, 2)
                wait(pe, yg_ready, i - 1, 1, 1)
                for t in range(NT):
                    for hg in range(NHG):
                        at = (t * NHG + hg) * VW
                        q0 = (hg % 2) * S + t * 128
                        last = nc.tensor.transpose(ps[:, W1, at:at + VW], o_t[:, hg // 2, q0:q0 + 128],
                                                   con[0:VW, C_ID:C_ID + VW])
                last.then_inc(ot_ps, 1)

            def transpose_on(i):
                wait(pe, on_ready, i, NT, NT)
                for t in range(NT):
                    last = nc.tensor.transpose(ps[:, W1, t * 128:(t + 1) * 128], o_n[:, t, :], ident)
                last.then_inc(ont_ps, 1)

            def output_projection(i):
                wait(pe, ont_ready, i, 1, 1)
                wait(pe, wog_ready, i, 1, 1)
                for t in range(NT):
                    last = nc.tensor.matmul(ps[:, W1, t * D:(t + 1) * D], on_t[:, t * 128:(t + 1) * 128],
                                            wo_g[:], start=True, stop=True)
                last.then_inc(wo_ps, 1)

            def step(i, pre, att, ffn):
                if att:
                    scores(i, 0)
                if ffn:
                    if pre:
                        wait(pe, v_ready, i, 2, 2)
                    transpose_norm(i - 1, xn2, xn2_ready, h2t_ps)
                if att:
                    scores(i, 1)
                if ffn:
                    logits(i - 1)
                if att:
                    subtract_max(i, 0)
                if ffn:
                    up(i - 1, 0)
                if att:
                    weigh_values(i, 0)
                    scores(i, 2)
                    subtract_max(i, 1)
                if ffn:
                    up(i - 1, 1)
                if att:
                    weigh_values(i, 1)
                    scores(i, 3)
                    subtract_max(i, 2)
                if ffn:
                    transpose_act(i - 1, 0)
                if att:
                    weigh_values(i, 2)
                    subtract_max(i, 3)
                if ffn:
                    transpose_act(i - 1, 1)
                if pre:
                    transpose_x(i + 1)
                if att:
                    weigh_values(i, 3)
                if ffn:
                    down(i - 1)
                if pre:
                    project_qk(i + 1)
                if att:
                    transpose_o(i)
                if pre:
                    project_v(i + 1, 0)
                if att:
                    transpose_on(i)
                if pre:
                    project_v(i + 1, 1)
                if att:
                    output_projection(i)

            pe.wait_ge(silu_step, 2)
            pe.wait_ge(mod_loaded, 32)
            for j in range(MODS):
                last = nc.tensor.matmul(ps[:, W0, j * B:(j + 1) * B], wm_sb[:, j * D:(j + 1) * D], silu_c[:],
                                        start=True, stop=True)
            last.then_inc(mod_ps, 1)
            pe.wait_ge(mod_step, 1)
            pe.wait_ge(consts_loaded, 16)
            transpose_x(0)
            pe.wait_ge(w_loaded, 9 * 16)
            project_qk(0)
            pe.wait_ge(mod_step, 6)
            for b in range(B):
                for w in range(2):
                    n = 2 * b + w
                    last = nc.tensor.matmul(ps[:, n // 4, (n % 4) * D:(n % 4 + 1) * D],
                                            view(gates[:, w, b:b + 1], [[0, 128]]), ident,
                                            start=True, stop=True)
                    if n == 8 or n == 15:
                        last.then_inc(gate_ps, 1)
            project_v(0, 0)
            project_v(0, 1)
            pe.wait_ge(gate_row_ready, 2)
            pe.wait_ge(consts_made, 5)
            steps(pe, step)

        @block.vector
        def _(dve):
            def norm_stats(b, xs, stats, stat, mv, var):
                for t in range(NT):
                    nc.vector.bn_stats(stats[:, t, :], xs[:, t, :]).then_inc(stat, 1)
                wait(dve, stat, b, NT, NT)
                for t in range(NT):
                    nc.vector.bn_aggr(mv[:, t, :], stats[:, t, :]).then_inc(var, 1)

            def normalise(b, xs, mv, rs, rs_ready, xn, ready):
                wait(dve, rs_ready, b, 1, 1)
                for t in range(NT):
                    nc.vector.tensor_scalar(xn[:, t, :], xs[:, t, :], mv[:, t, 0:1], rs[:, t:t + 1],
                                            ALU.subtract, ALU.mult).then_inc(ready, 1)

            def norm1(b):
                wait(dve, x_loaded, b, 16, 16)
                norm_stats(b, x_sb, stats1, ln1_stat, mv1, ln1_var)

            def norm1_apply(b):
                wait(dve, xt_ps, b, 1, 0)
                normalise(b, x_sb, mv1, rstd1, rstd1_ready, xn1, xn1_ready)

            def keep_k(b):
                wait(dve, qk_ps, b, 1, 1)
                wait(dve, q_ready, b, 1, 1)
                wait(dve, scores_ps, b, NHG, 0)
                nc.vector.tensor_tensor(k_bd[:], view(ps[:, W0, S:S + 1], [[KB, NKB], [0, G], [1, KB]]),
                                        view(con[:, C_HEAD:C_HEAD + 1], [[0, NKB], [1, G], [0, KB]]),
                                        ALU.mult).then_inc(k_ready, 1)

            def keep_v(b, half):
                wait(dve, v_ps, b, 2, half + 1)
                wait(dve, pv_ps, b, NHG, 0)
                nc.vector.tensor_tensor(
                    view(v_bd[:, half * BANKKB, 0, 0:1], [[VW, BANKKB * NHG], [1, G * DH]]),
                    view(ps[:, W0, 0:1], [[G * DH, BANKKB * NHG], [1, G * DH]]),
                    view(con[:, C_BD:C_BD + 1], [[0, BANKKB * NHG], [1, G * DH]]), ALU.mult).then_inc(v_ready, 1)

            def find_max(i, hg):
                half = hg % 2
                wait(dve, scores_ps, i, NHG, hg + 1)
                nc.vector.tensor_reduce(
                    blkmax[:, half, 1:1 + 3 * NKB],
                    view(ps[:, 2 * half, 0:1], [[BANK, 2], [KB, 3 * BANKKB], [1, KB]]),
                    AX.X, ALU.max, apply_transpose=True).then_inc(max_step, 1)
                wait(dve, max_step, i, 2 * NHG, 2 * hg + 1)
                nc.vector.tensor_reduce(row_max[:], view(blkmax[:, half, 0:1], [[3, NKB], [2, 3]]),
                                        AX.X, ALU.max).then_inc(max_step, 1)
                wait(dve, max_step, i, 2 * NHG, 2 * hg + 2)
                wait(dve, shifted_ps, i, NHG, hg - 1)
                nc.vector.tensor_tensor(
                    shift[:, half, HALF:HALF + S].rearrange("p (b q) -> p b q", b=NKB),
                    view(row_max[:], [[1, NKB], [0, KB]]),
                    view(con[:, C_NI:C_NI + 1], [[0, NKB], [1, KB]]), ALU.mult).then_inc(shift_ready, 1)

            def route(b):
                wait(dve, ex_ready, b, 1, 1)
                wait(dve, actw_ready, b, NT, 0)
                n = [0]

                def then(ins):
                    n[0] += 1
                    ins.then_inc(route_step, 1)
                    wait(dve, route_step, b, ROUTE, n[0])

                def before(dst_gt, dst_eq, dst_tie, dst_all, dst_rank, v, count, tie):
                    mine = view(v[:], [[count, NT], [1, count], [0, count]])
                    other = view(v[:], [[count, NT], [0, count], [1, count]])
                    nc.vector.tensor_tensor(dst_gt[:], other, mine, ALU.is_gt).then_inc(rank_gt, 1)
                    then(nc.vector.tensor_tensor(dst_eq[:], other, mine, ALU.is_equal))
                    then(nc.vector.tensor_tensor(
                        dst_tie[:].rearrange("p t a b -> p t (a b)"), dst_eq[:].rearrange("p t a b -> p t (a b)"),
                        view(con[:, tie:tie + 1], [[0, NT], [1, count * count]]), ALU.mult))
                    dve.wait_ge(rank_gt, b * 2 + (1 if count == NG else 2))
                    then(nc.vector.tensor_tensor(dst_all[:], dst_gt[:], dst_tie[:], ALU.add))
                    then(nc.vector.tensor_reduce(dst_rank[:].rearrange("p t a -> p (t a)"),
                                                 dst_all[:].rearrange("p t a b -> p (t a) b"), AX.X, ALU.add))

                flat = "p t e -> p (t e)"
                then(nc.vector.tensor_scalar(exp1[:], ex[:], 1.0, None, ALU.add))
                then(nc.vector.reciprocal(score[:], exp1[:]))
                then(nc.vector.tensor_tensor(choice[:], score[:], bias_sb[:], ALU.add))
                then(nc.vector.tensor_tensor(gsum[:], choice[:, :, 0::2], choice[:, :, 1::2], ALU.add))
                before(ggt, geq, gtie, gall, grank, gsum, NG, C_LG)
                then(nc.vector.scalar_tensor_tensor(
                    out=tmp[:].rearrange("p t (g e) -> p (t g) e", e=GSZ),
                    in0=view(grank[:], [[1, NT * NG], [0, GSZ]]), scalar=TOPKG - 0.5,
                    in1=choice[:].rearrange("p t (g e) -> p (t g) e", e=GSZ), op0=ALU.is_lt, op1=ALU.mult))
                before(egt, eeq, etie, eall, rank, tmp, E, C_LE)
                then(nc.vector.scalar_tensor_tensor(
                    out=wsel[:].rearrange(flat), in0=rank[:].rearrange(flat), scalar=TOPK - 0.5,
                    in1=score[:].rearrange(flat), op0=ALU.is_lt, op1=ALU.mult))
                then(nc.vector.tensor_reduce(wsum[:], wsel[:], AX.X, ALU.add))
                then(nc.vector.tensor_scalar(wsum2[:], wsum[:], 1e-20, 2.0, ALU.add, ALU.mult))
                then(nc.vector.reciprocal(rsum[:], wsum2[:]))
                nc.vector.tensor_tensor(cw[:], wsel[:], view(rsum[:], [[1, NT], [0, E]]), ALU.mult)\
                  .then_inc(cw_ready, 1)
                assert n[0] == ROUTE

            def activate(b, t):
                wait(dve, tanh_ready, b, NT, t + 1)
                nc.vector.scalar_tensor_tensor(out=gate_a[:], in0=tanh_g[:], scalar=1.0, in1=ps[:, W0, :],
                                               op0=ALU.add, op1=ALU.mult).then_inc(gate_a_ready, 1)
                wait(dve, gate_a_ready, b, NT, t + 1)
                wait(dve, actw_ready, b, NT, 0)
                nc.vector.tensor_tensor(act[:, t, :], gate_a[:], ps[:, W1, :], ALU.mult).then_inc(act_ready, 1)

            def step(i, pre, att, ffn):
                if att:
                    find_max(i, 0)
                    find_max(i, 1)
                if ffn:
                    route(i - 1)
                    activate(i - 1, 0)
                if att:
                    find_max(i, 2)
                if ffn:
                    activate(i - 1, 1)
                if pre:
                    norm1(i + 1)
                if att:
                    find_max(i, 3)
                if pre:
                    norm1_apply(i + 1)
                if ffn:
                    wait(dve, down_ps, i - 1, 1, 1)
                    wait(dve, out_ready, i - 1, 1, 0)
                    nc.vector.tensor_tensor(
                        y_g[:], ps[:, W1, 0:NT * D].rearrange("p (t d) -> p t d", t=NT),
                        view(gate_row[:, bass.ds(i - 1, 1), 1, :], [[0, NT], [1, D]]), ALU.mult)\
                      .then_inc(yg_ready, 1)
                if att:
                    wait(dve, ot_ps, i, 1, 1)
                    nc.vector.reciprocal(
                        rden[:].rearrange("p t (a g) -> p (t a) g", g=G),
                        view(ps[:, W1, G * DH:G * DH + 1], [[VW, NT * NHG], [1, G]])).then_inc(rden_ready, 1)
                if pre:
                    keep_k(i + 1)
                    keep_v(i + 1, 0)
                if att:
                    wait(dve, rden_ready, i, 1, 1)
                    for t in range(NT):
                        nc.vector.tensor_tensor(
                            o_n[:, t, :].rearrange("p (a g d) -> p a g d", a=NHG, g=G),
                            view(ps[:, W1, t * NHG * VW:t * NHG * VW + 1], [[VW, NHG], [DH, G], [1, DH]]),
                            view(rden[:, t, 0:1], [[G, NHG], [1, G], [0, DH]]), ALU.mult).then_inc(on_ready, 1)
                if pre:
                    keep_v(i + 1, 1)
                if att:
                    wait(dve, wo_ps, i, 1, 1)
                    wait(dve, xres_ready, i, 1, 1)
                    wait(dve, out_ready, i, 1, 0)
                    nc.vector.tensor_tensor(x1[:], ps[:, W1, 0:NT * D].rearrange("p (t d) -> p t d", t=NT),
                                            x_res[:], ALU.add).then_inc(x1_ready, 1)
                    wait(dve, x1_ready, i, 1, 1)
                    norm_stats(i, x1, stats2, ln2_stat, mv2, ln2_var)
                    wait(dve, h2t_ps, i, 1, 0)
                    normalise(i, x1, mv2, rstd2, rstd2_ready, xn2, xn2_ready)

            dve.memset(blkmax[:], -3e38).then_inc(consts_made, 1)
            dve.memset(shift[:].bitcast(F32), 0.0).then_inc(consts_made, 1)
            norm1(0)
            dve.wait_ge(tanh_c_ready, 1)
            nc.vector.scalar_tensor_tensor(out=silu2_c[:], in0=ct_t[:], scalar=1.0, in1=ct_sb[:],
                                           op0=ALU.add, op1=ALU.mult).then_inc(silu_step, 1)
            dve.wait_ge(silu_step, 1)
            nc.vector.tensor_scalar(silu_c[:], silu2_c[:], 0.5, None, ALU.mult).then_inc(silu_step, 1)
            norm1_apply(0)
            dve.wait_ge(mod_ps, 1)
            nc.vector.tensor_copy(mod[:].rearrange("p m b -> p (m b)"), ps[:, W0, 0:MODS * B]).then_inc(mod_step, 1)
            dve.wait_ge(mod_step, 1)
            nc.vector.tensor_scalar(mod[:, CA::3, :], mod[:, CA::3, :], 1.0, None, ALU.add).then_inc(mod_step, 1)
            nc.vector.tensor_scalar(gsign[:], mod[:, GA::3, :], 0.0, 2.0, ALU.is_ge, ALU.mult).then_inc(mod_step, 1)
            nc.vector.scalar_tensor_tensor(out=gabs[:], in0=mod[:, GA::3, :], scalar=-1.0, in1=mod[:, GA::3, :],
                                           op0=ALU.mult, op1=ALU.max).then_inc(mod_step, 1)
            dve.wait_ge(mod_step, 4)
            nc.vector.tensor_scalar(gsize[:], gabs[:], GATE_MIN, None, ALU.max).then_inc(mod_step, 1)
            dve.wait_ge(mod_step, 5)
            nc.vector.scalar_tensor_tensor(out=gates[:], in0=gsign[:], scalar=-1.0, in1=gsize[:],
                                           op0=ALU.add, op1=ALU.mult).then_inc(mod_step, 1)
            dve.wait_ge(consts_loaded, 16)
            nc.vector.tensor_copy(ident_bf[:], ident).then_inc(consts_made, 1)
            nc.vector.tensor_copy(mask_bf[:].rearrange("p a q -> p (a q)"),
                                  con[:, C_MASK:C_MASK + 2 * KB]).then_inc(consts_made, 1)
            nc.vector.tensor_copy(quad_ones[:], con[:, C_ONES:C_ONES + 128]).then_inc(consts_made, 1)
            dve.wait_ge(zeroed, 3)
            nc.vector.tensor_copy(view(v_bd[:, 0, 0, G * DH:G * DH + 1], [[VW, NKB * NHG], [1, G]]),
                                  view(con[:, C_DEN:C_DEN + 1], [[0, NKB * NHG], [1, G]])).then_inc(dens_made, 1)
            keep_k(0)
            keep_v(0, 0)
            keep_v(0, 1)
            dve.wait_ge(dens_made, 1)
            steps(dve, step)


def launch_inputs(a):
    t = np.ascontiguousarray
    wqkv = a["L0_attn_W_qkv"]
    up = lambda w: t(w.reshape(EI, D).T)
    return {
        "x": t(a["L0_attn_x"]),
        "wq": t(wqkv[0:D].T), "wk": t(wqkv[D:2 * D].T), "wv": t(wqkv[2 * D:3 * D].T),
        "wo": t(a["L0_attn_W_o"].T),
        "gate_w": t(a["L0_ffn_gate_weight"].T),
        "bias": t(np.broadcast_to(a["L0_ffn_e_score_correction_bias"], (128, NT, E))),
        "w_gate": up(a["L0_ffn_gate_proj"]), "w_up": up(a["L0_ffn_up_proj"]),
        "w_down": t(a["L0_ffn_down_proj"].transpose(0, 2, 1).reshape(NC_, 128, D).transpose(1, 0, 2)),
        "c_t": t(a["L0_c"].T), "wmod": t(a["L0_wmod"]),
        "consts": constants(),
    }


def kernel(**inputs):
    import concourse.bacc as bacc
    from concourse.bass_utils import run_bass_kernel_spmd

    nc = bacc.Bacc("TRN2", target_bir_lowering=False, num_devices=1)
    arrays = launch_inputs({k: np.asarray(v) for k, v in inputs.items()})
    aps = {k: nc.dram_tensor(k, v.shape, F32, kind="ExternalInput").ap() for k, v in arrays.items()}
    out = nc.dram_tensor("out", (B, S, D), F32, kind="ExternalOutput").ap()
    program(nc, out=out, **aps)
    return run_bass_kernel_spmd(nc, [arrays], core_ids=[0]).results[0]["out"]
```

```python
from contextlib import ExitStack

import numpy as np

import concourse.bass as bass
from concourse import mybir

ALU = mybir.AluOpType
ACT = mybir.ActivationFunctionType
AX = mybir.AxisListType
F32 = mybir.dt.float32
F32R = mybir.dt.float32r
BF16 = mybir.dt.bfloat16

B, S, D = 8, 256, 128
H, DH = 16, 8
HALF = 32
KB = 32
NKB = S // KB
WIN = KB + 2 * HALF
G = D // KB
NHG = H // G
BANKKB = 4
SC = BANKKB * WIN
VW = G * DH + G
OP = 64
XBUF = 4
E, I = 8, 64
NT = S // 128
EI = E * I
NC_ = EI // 128
NG, GSZ = 4, 2
TOPK = TOPKG = 2
EPS = 1e-5
GATE_MIN = 0.25
MASKED = -1e30
BANK = 512
ROUTE = 4 + 4 + 1 + 4 + 4
MODS = 6
SA, CA, GA, SB, CB, GB = range(MODS)

C_ID = 0
C_MASK = C_ID + 128
C_NI = C_MASK + 2 * KB
C_ONES = C_NI + KB
C_BD = C_ONES + 128
C_DEN = C_BD + G * DH
C_HEAD = C_DEN + G
C_LG = C_HEAD + G
C_LE = C_LG + NG * NG
C_END = C_LE + E * E


def constants():
    c = np.zeros((128, C_END), np.float32)
    p = np.arange(128)
    g, r = p // KB, p % KB
    c[:, C_ID:C_ID + 128] = np.eye(128)
    q = np.arange(KB)
    c[:, C_MASK:C_MASK + KB] = np.where(r[:, None] <= q[None], 0.0, MASKED)
    c[:, C_MASK + KB:C_MASK + 2 * KB] = np.where(q[None] <= r[:, None], 0.0, MASKED)
    c[:, C_NI:C_NI + KB] = np.where(r[:, None] == q[None], -1.0, 0.0)
    c[:, C_ONES:C_ONES + 128] = g[:, None] == g[None]
    c[:, C_BD:C_BD + G * DH] = g[:, None] == (np.arange(G * DH) // DH)[None]
    c[:, C_DEN:C_DEN + G] = g[:, None] == np.arange(G)[None]
    c[:, C_HEAD:C_HEAD + G] = (p // DH % G)[:, None] == np.arange(G)[None]
    c[:, C_LG:C_LG + NG * NG] = (np.arange(NG)[None] < np.arange(NG)[:, None]).reshape(1, -1)
    c[:, C_LE:C_LE + E * E] = (np.arange(E)[None] < np.arange(E)[:, None]).reshape(1, -1)
    return c


def view(ap, dims):
    return bass.AP(ap.tensor, ap.offset, [list(ap.ap[0])] + [list(d) for d in dims])


def program(nc, x, wq, wk, wv, wo, gate_w, bias, w_gate, w_up, w_down, c_t, wmod, consts, out):
    with ExitStack() as ctx:
        def sb(name, shape, dt=F32):
            return ctx.enter_context(nc.sbuf_tensor(name, shape, dt))

        def sem(name):
            return ctx.enter_context(nc.semaphore(name))

        con = sb("con", [128, C_END])
        wq_sb, wk_sb, wv_sb, wo_sb = (sb(n, [128, D]) for n in ("wq_sb", "wk_sb", "wv_sb", "wo_sb"))
        gw_sb = sb("gw_sb", [128, E])
        bias_sb = sb("bias_sb", [128, NT, E])
        wg_sb, wu_sb = sb("wg_sb", [128, EI]), sb("wu_sb", [128, EI])
        wd_sb = sb("wd_sb", [128, NC_, D])
        ct_sb = sb("ct_sb", [128, B])
        wm_sb = sb("wm_sb", [128, MODS * D])
        ct_t, silu2_c, silu_c = (sb(n, [128, B]) for n in ("ct_t", "silu2_c", "silu_c"))
        mod = sb("mod", [128, MODS, B])
        gsign, gabs, gsize = (sb(n, [128, 2, B]) for n in ("gsign", "gabs", "gsize"))
        gates = sb("gates", [128, 2, B])
        gate_row = sb("gate_row", [128, B, 2, D])
        ident_bf = sb("ident_bf", [128, 128], BF16)
        mask_bf = sb("mask_bf", [128, 2, KB], BF16)
        quad_ones = sb("quad_ones", [128, 128], F32R)
        minus_half = sb("minus_half", [128, NT])

        x_sb = sb("x_sb", [128, XBUF, NT, D])
        stats1, mv1 = sb("stats1", [128, NT, 6]), sb("mv1", [128, NT, 2])
        veps1, rstd1 = sb("veps1", [128, NT]), sb("rstd1", [128, NT])
        xn1 = sb("xn1", [128, NT, D])
        h_t = sb("h_t", [128, S])
        q_pad = sb("q_pad", [128, HALF + S + HALF])
        k_bd = sb("k_bd", [128, NKB, G, KB])
        h_rep = sb("h_rep", [128, NKB, G, KB])
        v_bd = sb("v_bd", [128, NKB, NHG, VW])

        blkmax = sb("blkmax", [128, 2, 3 * NKB + 2])
        row_max = sb("row_max", [128, NKB])
        shift = sb("shift", [128, 2, HALF + S + HALF], F32R)
        probs = sb("probs", [128, 2, 2 * SC])
        o_t = sb("o_t", [OP + VW, 2, S])
        rden = sb("rden", [128, NT, H])
        o_n, on_t = sb("o_n", [128, NT, D]), sb("on_t", [128, S])
        wo_g = sb("wo_g", [128, D])
        x1 = sb("x1", [128, 2, NT, D])

        stats2, mv2 = sb("stats2", [128, NT, 6]), sb("mv2", [128, NT, 2])
        veps2, rstd2 = sb("veps2", [128, NT]), sb("rstd2", [128, NT])
        xn2 = sb("xn2", [128, NT, D])
        h2_t = sb("h2_t", [128, S])
        ex = sb("ex", [128, NT, E])
        exp1, score, choice = (sb(n, [128, NT, E]) for n in ("exp1", "score", "choice"))
        gsum, grank = sb("gsum", [128, NT, NG]), sb("grank", [128, NT, NG])
        ggt, geq, gtie, gall = (sb(n, [128, NT, NG, NG]) for n in ("ggt", "geq", "gtie", "gall"))
        tmp, rank, wsel, cw = (sb(n, [128, NT, E]) for n in ("tmp", "rank", "wsel", "cw"))
        egt, eeq, etie, eall = (sb(n, [128, NT, E, E]) for n in ("egt", "eeq", "etie", "eall"))
        wsum, wsum2, rsum = (sb(n, [128, NT]) for n in ("wsum", "wsum2", "rsum"))
        tanh_g, gate_a = sb("tanh_g", [128, EI]), sb("gate_a", [128, EI])
        act, act_w = sb("act", [128, NT, EI]), sb("act_w", [128, NT, EI])
        act_t = sb("act_t", [128, NT, NC_, 128])
        y_g, out_sb = sb("y_g", [128, NT, D]), sb("out_sb", [128, NT, D])

        ps = ctx.enter_context(nc.psum_tensor("ps", [128, 8, BANK], F32))
        OB, W0, W1, W2 = 4, 5, 6, 7
        VBANK = (W2, W1)

        w_loaded, consts_loaded, mod_loaded = sem("w_loaded"), sem("consts_loaded"), sem("mod_loaded")
        zeroed, silu_step, mod_step, consts_made = sem("zeroed"), sem("silu_step"), sem("mod_step"), sem("consts_made")
        dens_made, rank_gt = sem("dens_made"), sem("rank_gt")
        tanh_c_ready, mod_ps, gate_ps, gate_row_ready = (
            sem("tanh_c_ready"), sem("mod_ps"), sem("gate_ps"), sem("gate_row_ready"))
        x_loaded = [sem(f"x_loaded{k}") for k in range(XBUF)]
        out_stored = sem("out_stored")
        xt_ps, qk_ps, v_ps = sem("xt_ps"), sem("qk_ps"), sem("v_ps")
        scores_ps, shifted_ps, pv_ps = sem("scores_ps"), sem("shifted_ps"), sem("pv_ps")
        ot_ps, ont_ps, wo_ps = sem("ot_ps"), sem("ont_ps"), sem("wo_ps")
        h2t_ps, logits_ps, up_ps, actt_ps, down_ps = (
            sem("h2t_ps"), sem("logits_ps"), sem("up_ps"), sem("actt_ps"), sem("down_ps"))
        ln1_stat, ln1_var, xn1_ready, v_ready = sem("ln1_stat"), sem("ln1_var"), sem("xn1_ready"), sem("v_ready")
        max_step, shift_ready = sem("max_step"), sem("shift_ready")
        rden_ready, on_ready, x1_ready, ln2_stat, ln2_var, xn2_ready = (
            sem("rden_ready"), sem("on_ready"), sem("x1_ready"), sem("ln2_stat"), sem("ln2_var"), sem("xn2_ready"))
        route_step, cw_ready, gate_a_ready, act_ready, yg_ready = (
            sem("route_step"), sem("cw_ready"), sem("gate_a_ready"), sem("act_ready"), sem("yg_ready"))
        h_ready, q_ready, k_ready, probs_ready, o_ready, ont_ready = (
            sem("h_ready"), sem("q_ready"), sem("k_ready"), sem("probs_ready"), sem("o_ready"), sem("ont_ready"))
        h2_ready, ex_ready, tanh_ready, actt_ready = (
            sem("h2_ready"), sem("ex_ready"), sem("tanh_ready"), sem("actt_ready"))
        eps1_step, rstd1_ready, eps2_step, rstd2_ready = (
            sem("eps1_step"), sem("rstd1_ready"), sem("eps2_step"), sem("rstd2_ready"))
        hrep_ready, wog_ready, actw_ready, out_ready = (
            sem("hrep_ready"), sem("wog_ready"), sem("actw_ready"), sem("out_ready"))

        def wait(eng, s, b, per, k):
            v = b * per + k
            if isinstance(v, int) and v <= 0:
                return
            eng.wait_ge(s, v)

        def steps(step):
            for i in range(B + 2):
                step(i, i + 1 < B, i < B, 1 <= i <= B, i >= 2)

        ident = con[:, C_ID:C_ID + 128]
        block = ctx.enter_context(nc.Block())

        @block.sync
        def _(sp):
            def load_x(b):
                wait(sp, x1_ready, b - XBUF, 1, 1)
                sp.dma_start(x_sb[:, b % XBUF], x[b].rearrange("(t p) d -> p t d", p=128)).then_inc(x_loaded[b % XBUF], 16)

            def step(i, pre, att, tail, ffn):
                if i + 2 < B:
                    load_x(i + 2)
                if ffn:
                    wait(sp, out_ready, i - 2, 1, 1)
                    sp.dma_start(out[i - 2].rearrange("(t p) d -> p t d", p=128), out_sb[:]).then_inc(out_stored, 16)

            load_x(0)
            for dst, src in ((con, consts),):
                sp.dma_start(dst[:], src).then_inc(consts_loaded, 16)
            for dst, src in ((wq_sb, wq), (wk_sb, wk), (wv_sb, wv), (wo_sb, wo), (gw_sb, gate_w),
                             (bias_sb, bias), (wg_sb, w_gate), (wu_sb, w_up), (wd_sb, w_down)):
                sp.dma_start(dst[:], src).then_inc(w_loaded, 16)
            load_x(1)
            steps(step)
            sp.wait_ge(out_stored, 16 * B)

        @block.gpsimd
        def _(pool):
            def norm_scale(b, var, mv, veps, step_done, rs, used, ready):
                wait(pool, var, b, NT, NT)
                nc.gpsimd.tensor_scalar(veps[:], mv[:, :, 1], EPS, None, ALU.add).then_inc(step_done, 1)
                wait(pool, step_done, b, 1, 1)
                wait(pool, used, b, NT, 0)
                nc.gpsimd.tensor_tensor(rs[:], veps[:], minus_half[:], ALU.pow).then_inc(ready, 1)

            def step(i, pre, att, tail, ffn):
                if tail:
                    wait(pool, wo_ps, i - 1, 1, 0)
                    nc.gpsimd.tensor_tensor(wo_g[:], wo_sb[:], gate_row[:, i - 1, 0, :], ALU.mult)\
                      .then_inc(wog_ready, 1)
                if ffn:
                    for t in range(NT):
                        wait(pool, cw_ready, i - 2, 1, 1)
                        wait(pool, act_ready, i - 2, NT, t + 1)
                        wait(pool, actt_ps, i - 2, NT, 0)
                        nc.gpsimd.tensor_tensor(
                            act_w[:, t, :].rearrange("p (e i) -> p e i", e=E),
                            act[:, t, :].rearrange("p (e i) -> p e i", e=E),
                            view(cw[:, t, :], [[1, E], [0, I]]), ALU.mult).then_inc(actw_ready, 1)
                if tail:
                    norm_scale(i - 1, ln2_var, mv2, veps2, eps2_step, rstd2, xn2_ready, rstd2_ready)
                if pre:
                    norm_scale(i + 1, ln1_var, mv1, veps1, eps1_step, rstd1, xn1_ready, rstd1_ready)
                if ffn:
                    wait(pool, yg_ready, i - 2, 1, 1)
                    wait(pool, out_stored, i - 2, 16, 0)
                    nc.gpsimd.tensor_tensor(out_sb[:], y_g[:], x1[:, i % 2], ALU.add).then_inc(out_ready, 1)

            nc.gpsimd.memset(minus_half[:], -0.5).then_inc(zeroed, 1)
            nc.gpsimd.memset(q_pad[:], 0.0).then_inc(zeroed, 1)
            nc.gpsimd.memset(v_bd[:], 0.0).then_inc(zeroed, 1)
            nc.gpsimd.memset(o_t[:], 0.0).then_inc(zeroed, 1)
            pool.wait_ge(zeroed, 4)
            norm_scale(0, ln1_var, mv1, veps1, eps1_step, rstd1, xn1_ready, rstd1_ready)
            pool.wait_ge(w_loaded, 9 * 16)
            pool.wait_ge(gate_row_ready, 2)
            steps(step)

        @block.scalar
        def _(act_e):
            def modulate_x(b):
                wait(act_e, xt_ps, b, 1, 1)
                wait(act_e, v_ps, b, 2, 0)
                nc.scalar.activation(h_t[:], ps[:, W0, 0:S], ACT.Identity, scale=mod[:, CA, b:b + 1],
                                     bias=mod[:, SA, b:b + 1]).then_inc(h_ready, 1)
                wait(act_e, h_ready, b, 1, 1)
                nc.scalar.activation(h_rep[:], view(h_t[:, 0:1], [[KB, NKB], [0, G], [1, KB]]), ACT.Copy)\
                  .then_inc(hrep_ready, 1)

            def keep_q(b):
                wait(act_e, qk_ps, b, 1, 1)
                wait(act_e, scores_ps, b, NHG, 0)
                nc.scalar.activation(q_pad[:, HALF:HALF + S], ps[:, W0, 0:S], ACT.Copy).then_inc(q_ready, 1)

            def exponentials(i, hg):
                wait(act_e, shifted_ps, i, NHG, hg + 1)
                wait(act_e, pv_ps, i, NHG, hg - 1)
                half = hg % 2
                nc.scalar.activation(probs[:, half, :].rearrange("p (b c) -> p b c", b=2),
                                     ps[:, 2 * half:2 * half + 2, 0:SC], ACT.Exp,
                                     scale=float(DH) ** -0.5).then_inc(probs_ready, 1)

            def keep_o(i):
                wait(act_e, pv_ps, i, NHG, NHG)
                wait(act_e, ot_ps, i, 1, 0)
                for p0 in (0, OP):
                    nc.scalar.activation(o_t[p0:p0 + VW].rearrange("p a q -> p (a q)"), ps[p0:p0 + VW, OB, :],
                                         ACT.Copy).then_inc(o_ready, 1)

            def tanh_gate(b, t):
                wait(act_e, up_ps, b, NT, t + 1)
                wait(act_e, gate_a_ready, b, NT, t)
                nc.scalar.activation(tanh_g[:], ps[:, W0, :], ACT.Tanh, scale=0.5).then_inc(tanh_ready, 1)

            def keep_act_t(b, t):
                wait(act_e, actt_ps, b, NT, t + 1)
                nc.scalar.activation(act_t[:, t].rearrange("p c n -> p (c n)"), ps[:, W0 + t, :],
                                     ACT.Copy).then_inc(actt_ready, 1)

            def step(i, pre, att, tail, ffn):
                if tail:
                    keep_o(i - 1)
                if ffn:
                    tanh_gate(i - 2, 0)
                if tail:
                    wait(act_e, ont_ps, i - 1, 1, 1)
                    nc.scalar.activation(on_t[:], ps[:, W2, 0:S], ACT.Copy).then_inc(ont_ready, 1)
                if att:
                    exponentials(i, 0)
                if ffn:
                    tanh_gate(i - 2, 1)
                if att:
                    exponentials(i, 1)
                if ffn:
                    keep_act_t(i - 2, 0)
                    keep_act_t(i - 2, 1)
                if tail:
                    wait(act_e, h2t_ps, i - 1, 1, 1)
                    wait(act_e, up_ps, i - 1, NT, 0)
                    nc.scalar.activation(h2_t[:], ps[:, W2, 0:S], ACT.Identity, scale=mod[:, CB, i - 1:i],
                                         bias=mod[:, SB, i - 1:i]).then_inc(h2_ready, 1)
                    wait(act_e, logits_ps, i - 1, 1, 1)
                    wait(act_e, route_step, i - 1, ROUTE, 0)
                    nc.scalar.activation(ex[:].rearrange("p t e -> p (t e)"), ps[:, W2, 0:NT * E], ACT.Exp,
                                         scale=-1.0).then_inc(ex_ready, 1)
                if att:
                    exponentials(i, 2)
                if pre:
                    modulate_x(i + 1)
                if att:
                    exponentials(i, 3)
                if pre:
                    keep_q(i + 1)

            act_e.dma_start(ct_sb[:], c_t).then_inc(mod_loaded, 16)
            act_e.dma_start(wm_sb[:], wmod).then_inc(mod_loaded, 16)
            nc.scalar.preload_act_table(ACT.Exp)
            act_e.wait_ge(mod_loaded, 32)
            nc.scalar.activation(ct_t[:], ct_sb[:], ACT.Tanh, scale=0.5).then_inc(tanh_c_ready, 1)
            act_e.wait_ge(mod_step, 6)
            modulate_x(0)
            act_e.wait_ge(zeroed, 4)
            keep_q(0)
            for half in range(2):
                act_e.wait_ge(gate_ps, 2)
                nc.scalar.activation(gate_row[:, 4 * half:4 * half + 4].rearrange("p b w d -> p (b w d)"),
                                     ps[:, 2 * half:2 * half + 2, :].rearrange("p b c -> p (b c)"),
                                     ACT.Copy).then_inc(gate_row_ready, 1)
            steps(step)

        @block.tensor
        def _(pe):
            def transpose_norm(b, bank, xn, ready, done):
                wait(pe, ready, b, NT, NT)
                for t in range(NT):
                    last = nc.tensor.transpose(ps[:, bank, t * 128:(t + 1) * 128], xn[:, t, :], ident)
                last.then_inc(done, 1)

            def transpose_x(b):
                wait(pe, actt_ready, b - 3, NT, 1)
                transpose_norm(b, W0, xn1, xn1_ready, xt_ps)

            def project_qk(b):
                wait(pe, h_ready, b, 1, 1)
                nc.tensor.matmul(ps[:, W0, 0:S], wq_sb[:], h_t[:], start=True, stop=True)
                nc.tensor.matmul(ps[:, W0, S:2 * S], wk_sb[:], h_t[:], start=True, stop=True)\
                  .then_inc(qk_ps, 1)

            def project_v(b, half):
                if half == 0:
                    wait(pe, hrep_ready, b, 1, 1)
                    wait(pe, ex_ready, b - 2, 1, 1)
                else:
                    wait(pe, yg_ready, b - 3, 1, 1)
                for j in range(BANKKB):
                    kb = half * BANKKB + j
                    last = nc.tensor.matmul(ps[:, VBANK[half], j * D:(j + 1) * D],
                                            h_rep[:, kb].rearrange("p g k -> p (g k)"), wv_sb[:],
                                            start=True, stop=True)
                last.then_inc(v_ps, 1)

            def scores(i, hg):
                half = hg % 2
                if hg == 0:
                    wait(pe, k_ready, i, 1, 1)
                    wait(pe, q_ready, i, 1, 1)
                wait(pe, probs_ready, i, NHG, hg - 1)
                rows = slice(G * DH * hg, G * DH * (hg + 1))
                for kb in range(NKB):
                    bank, j = 2 * half + kb // BANKKB, kb % BANKKB
                    nc.tensor.matmul(ps[:, bank, j * WIN:(j + 1) * WIN],
                                     k_bd[rows, kb].rearrange("p g k -> p (g k)"),
                                     q_pad[rows, kb * KB:kb * KB + WIN],
                                     start=(j == 0), stop=False, skip_group_check=True)
                for bank in (2 * half, 2 * half + 1):
                    last = nc.tensor.matmul(
                        view(ps[:, bank, 0:1], [[WIN, BANKKB], [2 * KB, 2], [1, KB]]), ident_bf[:],
                        view(mask_bf[:, 0, 0:1], [[0, BANKKB], [KB, 2], [1, KB]]),
                        start=False, stop=False, skip_group_check=True)
                last.then_inc(scores_ps, 1)

            def subtract_max(i, hg):
                half = hg % 2
                wait(pe, shift_ready, i, NHG, hg + 1)
                for j in range(2):
                    last = nc.tensor.matmul(
                        ps[:, 2 * half + j, 0:SC], quad_ones[:],
                        view(shift[:, half, j * BANKKB * KB:j * BANKKB * KB + 1], [[KB, BANKKB], [1, WIN]]),
                        start=False, stop=True, skip_group_check=True)
                last.then_inc(shifted_ps, 1)

            def weigh_values(i, hg):
                half = hg % 2
                wait(pe, probs_ready, i, NHG, hg + 1)
                if hg == 0:
                    wait(pe, v_ready, i, 2, 2)
                if hg == 0:
                    wait(pe, o_ready, i - 1, 2, 2)
                p0, c0 = OP * (hg % 2), S * (hg // 2)
                for kb in range(NKB):
                    lo, hi = max(0, (kb - 1) * KB), min(S, (kb + 2) * KB)
                    at = kb * WIN + lo - (kb - 1) * KB
                    last = nc.tensor.matmul(ps[p0:p0 + VW, OB, c0 + lo:c0 + hi],
                                            v_bd[:, kb, hg, :], probs[:, half, at:at + hi - lo],
                                            start=(hg < 2 and kb == 0), stop=(kb == NKB - 1),
                                            skip_group_check=True)
                last.then_inc(pv_ps, 1)

            def logits(b):
                wait(pe, h2_ready, b, 1, 1)
                for t in range(NT):
                    last = nc.tensor.matmul(ps[:, W2, t * E:(t + 1) * E], h2_t[:, t * 128:(t + 1) * 128],
                                            gw_sb[:], start=True, stop=True)
                last.then_inc(logits_ps, 1)

            def up(b, t):
                if t == 0:
                    if b + 2 < B:
                        wait(pe, k_ready, b + 2, 1, 1)
                        wait(pe, q_ready, b + 2, 1, 1)
                        wait(pe, v_ready, b + 2, 2, 2)
                    wait(pe, h2_ready, b, 1, 1)
                    wait(pe, yg_ready, b - 1, 1, 1)
                else:
                    wait(pe, act_ready, b, NT, t)
                h2 = h2_t[:, t * 128:(t + 1) * 128]
                nc.tensor.matmul(ps[:, W0, :], h2, wg_sb[:], start=True, stop=True)
                nc.tensor.matmul(ps[:, W1, :], h2, wu_sb[:], start=True, stop=True).then_inc(up_ps, 1)

            def transpose_act(b, t):
                wait(pe, actw_ready, b, NT, t + 1)
                wait(pe, act_ready, b, NT, NT)
                for c in range(NC_):
                    last = nc.tensor.transpose(ps[:, W0 + t, c * 128:(c + 1) * 128],
                                               act_w[:, t, c * 128:(c + 1) * 128], ident)
                last.then_inc(actt_ps, 1)

            def down(b):
                wait(pe, actt_ready, b, NT, NT)
                for t in range(NT):
                    for c in range(NC_):
                        last = nc.tensor.matmul(ps[:, W1, t * D:(t + 1) * D], act_t[:, t, c, :],
                                                wd_sb[:, c, :], start=(c == 0), stop=(c == NC_ - 1))
                last.then_inc(down_ps, 1)

            def transpose_o(i):
                wait(pe, o_ready, i, 2, 2)
                if i + 1 < B:
                    wait(pe, v_ready, i + 1, 2, 1)
                for t in range(NT):
                    for pair in range(2):
                        at = (t * 2 + pair) * 128
                        last = nc.tensor.transpose(ps[:, W2, at:at + OP + VW], o_t[:, pair, t * 128:(t + 1) * 128],
                                                   con[0:OP + VW, C_ID:C_ID + OP + VW])
                last.then_inc(ot_ps, 1)

            def transpose_on(i):
                wait(pe, on_ready, i, 1, 1)
                for t in range(NT):
                    last = nc.tensor.transpose(ps[:, W2, t * 128:(t + 1) * 128], o_n[:, t, :], ident)
                last.then_inc(ont_ps, 1)

            def output_projection(i):
                wait(pe, ont_ready, i, 1, 1)
                wait(pe, wog_ready, i, 1, 1)
                for t in range(NT):
                    last = nc.tensor.matmul(ps[:, W2, t * D:(t + 1) * D], on_t[:, t * 128:(t + 1) * 128],
                                            wo_g[:], start=True, stop=True)
                last.then_inc(wo_ps, 1)

            def transpose_x1(i):
                wait(pe, x1_ready, i, 1, 1)
                transpose_norm(i, W2, xn2, xn2_ready, h2t_ps)

            def step(i, pre, att, tail, ffn):
                if att:
                    scores(i, 0)
                if tail:
                    transpose_o(i - 1)
                if ffn:
                    up(i - 2, 0)
                if att:
                    scores(i, 1)
                if tail:
                    transpose_on(i - 1)
                if att:
                    subtract_max(i, 0)
                if ffn:
                    up(i - 2, 1)
                if tail:
                    output_projection(i - 1)
                if att:
                    weigh_values(i, 0)
                    scores(i, 2)
                    subtract_max(i, 1)
                if ffn:
                    transpose_act(i - 2, 0)
                    transpose_act(i - 2, 1)
                if att:
                    weigh_values(i, 1)
                if tail:
                    transpose_x1(i - 1)
                if att:
                    scores(i, 3)
                if tail:
                    logits(i - 1)
                if att:
                    subtract_max(i, 2)
                if ffn:
                    down(i - 2)
                if pre:
                    transpose_x(i + 1)
                if att:
                    weigh_values(i, 2)
                    subtract_max(i, 3)
                if pre:
                    project_qk(i + 1)
                if att:
                    weigh_values(i, 3)
                if pre:
                    project_v(i + 1, 0)
                    project_v(i + 1, 1)

            pe.wait_ge(silu_step, 2)
            pe.wait_ge(mod_loaded, 32)
            for j in range(MODS):
                last = nc.tensor.matmul(ps[:, W0, j * B:(j + 1) * B], wm_sb[:, j * D:(j + 1) * D], silu_c[:],
                                        start=True, stop=True)
            last.then_inc(mod_ps, 1)
            pe.wait_ge(mod_step, 1)
            pe.wait_ge(consts_loaded, 16)
            transpose_x(0)
            pe.wait_ge(w_loaded, 9 * 16)
            project_qk(0)
            pe.wait_ge(mod_step, 6)
            for b in range(B):
                for w in range(2):
                    n = 2 * b + w
                    last = nc.tensor.matmul(ps[:, n // 4, (n % 4) * D:(n % 4 + 1) * D],
                                            view(gates[:, w, b:b + 1], [[0, 128]]), ident,
                                            start=True, stop=True)
                    if n == 8 or n == 15:
                        last.then_inc(gate_ps, 1)
            project_v(0, 0)
            project_v(0, 1)
            pe.wait_ge(gate_row_ready, 2)
            pe.wait_ge(consts_made, 5)
            steps(step)

        @block.vector
        def _(dve):
            def norm_stats(b, xs, stats, stat, mv, var):
                for t in range(NT):
                    nc.vector.bn_stats(stats[:, t, :], xs[:, t, :]).then_inc(stat, 1)
                wait(dve, stat, b, NT, NT)
                for t in range(NT):
                    nc.vector.bn_aggr(mv[:, t, :], stats[:, t, :]).then_inc(var, 1)

            def normalise(b, xs, mv, rs, rs_ready, xn, ready):
                wait(dve, rs_ready, b, 1, 1)
                for t in range(NT):
                    nc.vector.tensor_scalar(xn[:, t, :], xs[:, t, :], mv[:, t, 0:1], rs[:, t:t + 1],
                                            ALU.subtract, ALU.mult).then_inc(ready, 1)

            def norm1(b):
                wait(dve, x_loaded[b % XBUF], b // XBUF, 16, 16)
                norm_stats(b, x_sb[:, b % XBUF], stats1, ln1_stat, mv1, ln1_var)

            def norm1_apply(b):
                wait(dve, xt_ps, b, 1, 0)
                normalise(b, x_sb[:, b % XBUF], mv1, rstd1, rstd1_ready, xn1, xn1_ready)

            def keep_k(b):
                wait(dve, qk_ps, b, 1, 1)
                wait(dve, q_ready, b, 1, 1)
                wait(dve, scores_ps, b, NHG, 0)
                nc.vector.tensor_tensor(k_bd[:], view(ps[:, W0, S:S + 1], [[KB, NKB], [0, G], [1, KB]]),
                                        view(con[:, C_HEAD:C_HEAD + 1], [[0, NKB], [1, G], [0, KB]]),
                                        ALU.mult).then_inc(k_ready, 1)

            def keep_v(b, half):
                wait(dve, v_ps, b, 2, half + 1)
                wait(dve, pv_ps, b, NHG, 0)
                nc.vector.tensor_tensor(
                    view(v_bd[:, half * BANKKB, 0, 0:1], [[VW, BANKKB * NHG], [1, G * DH]]),
                    view(ps[:, VBANK[half], 0:1], [[G * DH, BANKKB * NHG], [1, G * DH]]),
                    view(con[:, C_BD:C_BD + 1], [[0, BANKKB * NHG], [1, G * DH]]), ALU.mult).then_inc(v_ready, 1)

            def find_max(i, hg):
                half = hg % 2
                wait(dve, scores_ps, i, NHG, hg + 1)
                nc.vector.tensor_reduce(
                    blkmax[:, half, 1:1 + 3 * NKB],
                    view(ps[:, 2 * half, 0:1], [[BANK, 2], [KB, 3 * BANKKB], [1, KB]]),
                    AX.X, ALU.max, apply_transpose=True).then_inc(max_step, 1)
                wait(dve, max_step, i, 2 * NHG, 2 * hg + 1)
                nc.vector.tensor_reduce(row_max[:], view(blkmax[:, half, 0:1], [[3, NKB], [2, 3]]),
                                        AX.X, ALU.max).then_inc(max_step, 1)
                wait(dve, max_step, i, 2 * NHG, 2 * hg + 2)
                wait(dve, shifted_ps, i, NHG, hg - 1)
                nc.vector.tensor_tensor(
                    shift[:, half, HALF:HALF + S].rearrange("p (b q) -> p b q", b=NKB),
                    view(row_max[:], [[1, NKB], [0, KB]]),
                    view(con[:, C_NI:C_NI + 1], [[0, NKB], [1, KB]]), ALU.mult).then_inc(shift_ready, 1)

            def route(b):
                wait(dve, ex_ready, b, 1, 1)
                wait(dve, actw_ready, b, NT, 0)
                n = [0]

                def then(ins):
                    n[0] += 1
                    ins.then_inc(route_step, 1)
                    wait(dve, route_step, b, ROUTE, n[0])

                def before(dst_gt, dst_eq, dst_tie, dst_all, dst_rank, v, count, tie):
                    mine = view(v[:], [[count, NT], [1, count], [0, count]])
                    other = view(v[:], [[count, NT], [0, count], [1, count]])
                    nc.vector.tensor_tensor(dst_gt[:], other, mine, ALU.is_gt).then_inc(rank_gt, 1)
                    then(nc.vector.tensor_tensor(dst_eq[:], other, mine, ALU.is_equal))
                    then(nc.vector.tensor_tensor(
                        dst_tie[:].rearrange("p t a b -> p t (a b)"), dst_eq[:].rearrange("p t a b -> p t (a b)"),
                        view(con[:, tie:tie + 1], [[0, NT], [1, count * count]]), ALU.mult))
                    dve.wait_ge(rank_gt, b * 2 + (1 if count == NG else 2))
                    then(nc.vector.tensor_tensor(dst_all[:], dst_gt[:], dst_tie[:], ALU.add))
                    then(nc.vector.tensor_reduce(dst_rank[:].rearrange("p t a -> p (t a)"),
                                                 dst_all[:].rearrange("p t a b -> p (t a) b"), AX.X, ALU.add))

                flat = "p t e -> p (t e)"
                then(nc.vector.tensor_scalar(exp1[:], ex[:], 1.0, None, ALU.add))
                then(nc.vector.reciprocal(score[:], exp1[:]))
                then(nc.vector.tensor_tensor(choice[:], score[:], bias_sb[:], ALU.add))
                then(nc.vector.tensor_tensor(gsum[:], choice[:, :, 0::2], choice[:, :, 1::2], ALU.add))
                before(ggt, geq, gtie, gall, grank, gsum, NG, C_LG)
                then(nc.vector.scalar_tensor_tensor(
                    out=tmp[:].rearrange("p t (g e) -> p (t g) e", e=GSZ),
                    in0=view(grank[:], [[1, NT * NG], [0, GSZ]]), scalar=TOPKG - 0.5,
                    in1=choice[:].rearrange("p t (g e) -> p (t g) e", e=GSZ), op0=ALU.is_lt, op1=ALU.mult))
                before(egt, eeq, etie, eall, rank, tmp, E, C_LE)
                then(nc.vector.scalar_tensor_tensor(
                    out=wsel[:].rearrange(flat), in0=rank[:].rearrange(flat), scalar=TOPK - 0.5,
                    in1=score[:].rearrange(flat), op0=ALU.is_lt, op1=ALU.mult))
                then(nc.vector.tensor_reduce(wsum[:], wsel[:], AX.X, ALU.add))
                then(nc.vector.tensor_scalar(wsum2[:], wsum[:], 1e-20, 2.0, ALU.add, ALU.mult))
                then(nc.vector.reciprocal(rsum[:], wsum2[:]))
                nc.vector.tensor_tensor(cw[:], wsel[:], view(rsum[:], [[1, NT], [0, E]]), ALU.mult)\
                  .then_inc(cw_ready, 1)
                assert n[0] == ROUTE

            def activate(b, t):
                wait(dve, tanh_ready, b, NT, t + 1)
                nc.vector.scalar_tensor_tensor(out=gate_a[:], in0=tanh_g[:], scalar=1.0, in1=ps[:, W0, :],
                                               op0=ALU.add, op1=ALU.mult).then_inc(gate_a_ready, 1)
                wait(dve, gate_a_ready, b, NT, t + 1)
                wait(dve, actw_ready, b, NT, 0)
                nc.vector.tensor_tensor(act[:, t, :], gate_a[:], ps[:, W1, :], ALU.mult).then_inc(act_ready, 1)

            def normalise_o(i):
                wait(dve, ot_ps, i, 1, 1)
                nc.vector.reciprocal(
                    rden[:].rearrange("p t (a g) -> p (t a) g", g=G),
                    view(ps[:, W2, G * DH:G * DH + 1], [[OP, NT * NHG], [1, G]])).then_inc(rden_ready, 1)
                wait(dve, rden_ready, i, 1, 1)
                nc.vector.tensor_tensor(
                    o_n[:].rearrange("p t (a g d) -> p (t a) g d", a=NHG, g=G),
                    view(ps[:, W2, 0:1], [[OP, NT * NHG], [DH, G], [1, DH]]),
                    view(rden[:, 0, 0:1], [[G, NT * NHG], [1, G], [0, DH]]), ALU.mult).then_inc(on_ready, 1)

            def residual(i):
                wait(dve, wo_ps, i, 1, 1)
                wait(dve, out_ready, i - 2, 1, 1)
                nc.vector.tensor_tensor(x1[:, i % 2], ps[:, W2, 0:NT * D].rearrange("p (t d) -> p t d", t=NT),
                                        x_sb[:, i % XBUF], ALU.add).then_inc(x1_ready, 1)
                wait(dve, x1_ready, i, 1, 1)
                norm_stats(i, x1[:, i % 2], stats2, ln2_stat, mv2, ln2_var)

            def gate_output(b):
                wait(dve, down_ps, b, 1, 1)
                wait(dve, out_ready, b, 1, 0)
                nc.vector.tensor_tensor(
                    y_g[:], ps[:, W1, 0:NT * D].rearrange("p (t d) -> p t d", t=NT),
                    view(gate_row[:, b, 1, :], [[0, NT], [1, D]]), ALU.mult).then_inc(yg_ready, 1)

            def step(i, pre, att, tail, ffn):
                if att:
                    find_max(i, 0)
                if tail:
                    normalise_o(i - 1)
                if ffn:
                    activate(i - 2, 0)
                if att:
                    find_max(i, 1)
                if ffn:
                    activate(i - 2, 1)
                if tail:
                    residual(i - 1)
                if att:
                    find_max(i, 2)
                if tail:
                    wait(dve, h2t_ps, i - 1, 1, 0)
                    normalise(i - 1, x1[:, (i - 1) % 2], mv2, rstd2, rstd2_ready, xn2, xn2_ready)
                if pre:
                    norm1(i + 1)
                if att:
                    find_max(i, 3)
                if pre:
                    norm1_apply(i + 1)
                if tail:
                    route(i - 1)
                if ffn:
                    gate_output(i - 2)
                if pre:
                    keep_k(i + 1)
                    keep_v(i + 1, 0)
                    keep_v(i + 1, 1)

            dve.memset(blkmax[:], -3e38).then_inc(consts_made, 1)
            dve.memset(shift[:].bitcast(F32), 0.0).then_inc(consts_made, 1)
            norm1(0)
            dve.wait_ge(tanh_c_ready, 1)
            nc.vector.scalar_tensor_tensor(out=silu2_c[:], in0=ct_t[:], scalar=1.0, in1=ct_sb[:],
                                           op0=ALU.add, op1=ALU.mult).then_inc(silu_step, 1)
            dve.wait_ge(silu_step, 1)
            nc.vector.tensor_scalar(silu_c[:], silu2_c[:], 0.5, None, ALU.mult).then_inc(silu_step, 1)
            norm1_apply(0)
            dve.wait_ge(mod_ps, 1)
            nc.vector.tensor_copy(mod[:].rearrange("p m b -> p (m b)"), ps[:, W0, 0:MODS * B]).then_inc(mod_step, 1)
            dve.wait_ge(mod_step, 1)
            nc.vector.tensor_scalar(mod[:, CA::3, :], mod[:, CA::3, :], 1.0, None, ALU.add).then_inc(mod_step, 1)
            nc.vector.tensor_scalar(gsign[:], mod[:, GA::3, :], 0.0, 2.0, ALU.is_ge, ALU.mult).then_inc(mod_step, 1)
            nc.vector.scalar_tensor_tensor(out=gabs[:], in0=mod[:, GA::3, :], scalar=-1.0, in1=mod[:, GA::3, :],
                                           op0=ALU.mult, op1=ALU.max).then_inc(mod_step, 1)
            dve.wait_ge(mod_step, 4)
            nc.vector.tensor_scalar(gsize[:], gabs[:], GATE_MIN, None, ALU.max).then_inc(mod_step, 1)
            dve.wait_ge(mod_step, 5)
            nc.vector.scalar_tensor_tensor(out=gates[:], in0=gsign[:], scalar=-1.0, in1=gsize[:],
                                           op0=ALU.add, op1=ALU.mult).then_inc(mod_step, 1)
            dve.wait_ge(consts_loaded, 16)
            nc.vector.tensor_copy(ident_bf[:], ident).then_inc(consts_made, 1)
            nc.vector.tensor_copy(mask_bf[:].rearrange("p a q -> p (a q)"),
                                  con[:, C_MASK:C_MASK + 2 * KB]).then_inc(consts_made, 1)
            nc.vector.tensor_copy(quad_ones[:], con[:, C_ONES:C_ONES + 128]).then_inc(consts_made, 1)
            dve.wait_ge(zeroed, 4)
            nc.vector.tensor_copy(view(v_bd[:, 0, 0, G * DH:G * DH + 1], [[VW, NKB * NHG], [1, G]]),
                                  view(con[:, C_DEN:C_DEN + 1], [[0, NKB * NHG], [1, G]])).then_inc(dens_made, 1)
            keep_k(0)
            keep_v(0, 0)
            keep_v(0, 1)
            dve.wait_ge(dens_made, 1)
            steps(step)


def launch_inputs(a):
    t = np.ascontiguousarray
    wqkv = a["L0_attn_W_qkv"]
    up = lambda w: t(w.reshape(EI, D).T)
    return {
        "x": t(a["L0_attn_x"]),
        "wq": t(wqkv[0:D].T), "wk": t(wqkv[D:2 * D].T), "wv": t(wqkv[2 * D:3 * D].T),
        "wo": t(a["L0_attn_W_o"].T),
        "gate_w": t(a["L0_ffn_gate_weight"].T),
        "bias": t(np.broadcast_to(a["L0_ffn_e_score_correction_bias"], (128, NT, E))),
        "w_gate": up(a["L0_ffn_gate_proj"]), "w_up": up(a["L0_ffn_up_proj"]),
        "w_down": t(a["L0_ffn_down_proj"].transpose(0, 2, 1).reshape(NC_, 128, D).transpose(1, 0, 2)),
        "c_t": t(a["L0_c"].T), "wmod": t(a["L0_wmod"]),
        "consts": constants(),
    }


def kernel(**inputs):
    import concourse.bacc as bacc
    from concourse.bass_utils import run_bass_kernel_spmd

    nc = bacc.Bacc("TRN2", target_bir_lowering=False, num_devices=1)
    arrays = launch_inputs({k: np.asarray(v) for k, v in inputs.items()})
    aps = {k: nc.dram_tensor(k, v.shape, F32, kind="ExternalInput").ap() for k, v in arrays.items()}
    out = nc.dram_tensor("out", (B, S, D), F32, kind="ExternalOutput").ap()
    program(nc, out=out, **aps)
    return run_bass_kernel_spmd(nc, [arrays], core_ids=[0]).results[0]["out"]
```

```python
from contextlib import ExitStack

import numpy as np

import concourse.bass as bass
from concourse import mybir

ALU = mybir.AluOpType
ACT = mybir.ActivationFunctionType
AX = mybir.AxisListType
F32 = mybir.dt.float32
F32R = mybir.dt.float32r
BF16 = mybir.dt.bfloat16

B, S, D = 8, 256, 128
H, DH = 16, 8
HALF = 32
KB = 32
NKB = S // KB
WIN = KB + 2 * HALF
G = D // KB
NHG = H // G
PAIR = 2
NPAIR = NHG // PAIR
BANKKB = 2
SC = BANKKB * PAIR * WIN
HALVES = 2
HB = NKB // BANKKB // HALVES
PAD = 4
PARTS = NPAIR * HALVES
NSRC = 128 // KB
VW = G * DH + G
OP = 64
XBUF = 4
E, I = 8, 64
NT = S // 128
EI = E * I
NC_ = EI // 128
NG, GSZ = 4, 2
TOPK = TOPKG = 2
EPS = 1e-5
GATE_MIN = 0.25
MASKED = -1e30
BANK = 512
COMPARE_STEPS = 4 + 1 + 3 + 1 + 1
ROUTE = COMPARE_STEPS + 3 + 4
MODS = 6
SA, CA, GA, SB, CB, GB = range(MODS)

C_ID = 0
C_MASK = C_ID + 128
C_NI = C_MASK + 2 * KB
C_ONES = C_NI + KB
C_DEN = C_ONES + 128
C_HEAD = C_DEN + G
C_LG = C_HEAD + G
C_LE = C_LG + NG * NG
C_END = C_LE + E * E


def constants():
    c = np.zeros((128, C_END), np.float32)
    p = np.arange(128)
    g, r = p // KB, p % KB
    c[:, C_ID:C_ID + 128] = np.eye(128)
    q = np.arange(KB)
    c[:, C_MASK:C_MASK + KB] = np.where(r[:, None] <= q[None], 0.0, MASKED)
    c[:, C_MASK + KB:C_MASK + 2 * KB] = np.where(q[None] <= r[:, None], 0.0, MASKED)
    c[:, C_NI:C_NI + KB] = np.where(r[:, None] == q[None], -1.0, 0.0)
    c[:, C_ONES:C_ONES + 128] = g[:, None] == g[None]
    c[:, C_DEN:C_DEN + G] = g[:, None] == np.arange(G)[None]
    c[:, C_HEAD:C_HEAD + G] = (p // DH % G)[:, None] == np.arange(G)[None]
    c[:, C_LG:C_LG + NG * NG] = (np.arange(NG)[None] < np.arange(NG)[:, None]).reshape(1, -1)
    c[:, C_LE:C_LE + E * E] = (np.arange(E)[None] < np.arange(E)[:, None]).reshape(1, -1)
    return c


def view(ap, dims):
    return bass.AP(ap.tensor, ap.offset, [list(ap.ap[0])] + [list(d) for d in dims])


def program(nc, x, wqkv, wo, gate_w, bias, w_gu, w_down, c_t, wmod, consts, out):
    with ExitStack() as ctx:
        def sb(name, shape, dt=F32):
            return ctx.enter_context(nc.sbuf_tensor(name, shape, dt))

        def sem(name):
            return ctx.enter_context(nc.semaphore(name))

        con = sb("con", [128, C_END])
        wqkv_sb, wo_sb = sb("wqkv_sb", [128, 3, D]), sb("wo_sb", [128, D])
        gw_sb = sb("gw_sb", [128, E])
        bias_sb = sb("bias_sb", [128, NT, E])
        wgu_sb = sb("wgu_sb", [128, 2, EI])
        wd_sb = sb("wd_sb", [128, NC_, D])
        ct_sb = sb("ct_sb", [128, B])
        wm_sb = sb("wm_sb", [128, MODS * D])
        ct_t, silu2_c, silu_c = (sb(n, [128, B]) for n in ("ct_t", "silu2_c", "silu_c"))
        mod = sb("mod", [128, MODS, B])
        gsign, gabs, gsize = (sb(n, [128, 2, B]) for n in ("gsign", "gabs", "gsize"))
        gates = sb("gates", [128, 2, B])
        gate_row = sb("gate_row", [128, B, 2, D])
        ident_bf = sb("ident_bf", [128, 128], BF16)
        mask_bf = sb("mask_bf", [128, 2, KB], BF16)
        quad_ones = sb("quad_ones", [128, 128], F32R)
        minus_half = sb("minus_half", [128, NT])

        x_sb = sb("x_sb", [128, XBUF, NT, D])
        stats1, mv1 = sb("stats1", [128, NT, 6]), sb("mv1", [128, NT, 2])
        veps1, rstd1 = sb("veps1", [128, NT]), sb("rstd1", [128, NT])
        xn1 = sb("xn1", [128, NT, D])
        h_t = sb("h_t", [128, S])
        q_pad = sb("q_pad", [128, NHG, HALF + S + HALF])
        k_bd = sb("k_bd", [128, NKB, G, KB])
        v_bd = sb("v_bd", [128, NKB, NHG, VW])

        blkmax = sb("blkmax", [128, PAD + NKB * PAIR * 3 + PAD])
        row_max = sb("row_max", [128, NKB, PAIR])
        shift = sb("shift", [128, PAIR, HALF + S + HALF], F32R)
        probs = sb("probs", [128, NPAIR, NKB // BANKKB, SC])
        o_t = sb("o_t", [OP + VW, 2, S])
        rden = sb("rden", [128, NT, H])
        o_n, on_t = sb("o_n", [128, NT, D]), sb("on_t", [128, S])
        wo_g = sb("wo_g", [128, D])
        x1 = sb("x1", [128, 2, NT, D])

        stats2, mv2 = sb("stats2", [128, NT, 6]), sb("mv2", [128, NT, 2])
        veps2, rstd2 = sb("veps2", [128, NT]), sb("rstd2", [128, NT])
        xn2 = sb("xn2", [128, NT, D])
        h2_t = sb("h2_t", [128, S])
        h2_hi, h2_lo = sb("h2_hi", [128, S], F32R), sb("h2_lo", [128, S], F32R)
        w_hi, w_lo = sb("w_hi", [128, 2, EI], F32R), sb("w_lo", [128, 2, EI], F32R)
        ex = sb("ex", [128, NT, E])
        exp1, score, choice = (sb(n, [128, NT, E]) for n in ("exp1", "score", "choice"))
        gsum, grank = sb("gsum", [128, NT, NG]), sb("grank", [128, NT, NG])
        ggt, geq, gtie, gall = (sb(n, [128, NT, NG, NG]) for n in ("ggt", "geq", "gtie", "gall"))
        tmp, rank, wsel, cw = (sb(n, [128, NT, E]) for n in ("tmp", "rank", "wsel", "cw"))
        egt, eeq, etie, eall = (sb(n, [128, NT, E, E]) for n in ("egt", "eeq", "etie", "eall"))
        wsum, wsum2, rsum = (sb(n, [128, NT]) for n in ("wsum", "wsum2", "rsum"))
        tanh_g, gate_a = sb("tanh_g", [128, EI]), sb("gate_a", [128, EI])
        act, act_w = sb("act", [128, NT, EI]), sb("act_w", [128, NT, EI])
        act_t = sb("act_t", [128, NT, NC_, 128])
        y_g, out_sb = sb("y_g", [128, NT, D]), sb("out_sb", [128, NT, D])
        y_last, out_last = sb("y_last", [128, NT, D]), sb("out_last", [128, NT, D])

        ps = ctx.enter_context(nc.psum_tensor("ps", [128, 8, BANK], F32))
        OB, W0, W1, W2 = 4, 5, 6, 7

        c_loaded, mod1_loaded, mod_loaded, consts_loaded, qkv_loaded, w_loaded = (
            sem("c_loaded"), sem("mod1_loaded"), sem("mod_loaded"), sem("consts_loaded"), sem("qkv_loaded"),
            sem("w_loaded"))
        mod1_ready = sem("mod1_ready")
        zeroed, silu_step, mod_step, consts_made = sem("zeroed"), sem("silu_step"), sem("mod_step"), sem("consts_made")
        w_parts = sem("w_parts")
        dens_made, rank_gt = sem("dens_made"), sem("rank_gt")
        tanh_c_ready, mod_ps, gate_ps, gate_row_ready = (
            sem("tanh_c_ready"), sem("mod_ps"), sem("gate_ps"), sem("gate_row_ready"))
        x_loaded = [sem(f"x_loaded{k}") for k in range(XBUF)]
        out_stored, last_ready = sem("out_stored"), sem("last_ready")
        xt_ps, qk_ps, v_ps = sem("xt_ps"), sem("qk_ps"), sem("v_ps")
        scores_ps, shifted_ps, pv_ps = sem("scores_ps"), sem("shifted_ps"), sem("pv_ps")
        ot_ps, ont_ps, wo_ps = sem("ot_ps"), sem("ont_ps"), sem("wo_ps")
        h2t_ps, logits_ps, up_ps, actt_ps, down_ps = (
            sem("h2t_ps"), sem("logits_ps"), sem("up_ps"), sem("actt_ps"), sem("down_ps"))
        ln1_stat, ln1_var, xn1_ready = sem("ln1_stat"), sem("ln1_var"), sem("xn1_ready")
        blkmax_ready, rowmax_ready, shift_ready = sem("blkmax_ready"), sem("rowmax_ready"), sem("shift_ready")
        rden_ready, on_ready, x1_ready, ln2_stat, ln2_var, xn2_ready = (
            sem("rden_ready"), sem("on_ready"), sem("x1_ready"), sem("ln2_stat"), sem("ln2_var"), sem("xn2_ready"))
        route_step, cw_ready, gate_a_ready, act_ready, yg_ready = (
            sem("route_step"), sem("cw_ready"), sem("gate_a_ready"), sem("act_ready"), sem("yg_ready"))
        h_ready, q_ready, k_ready, probs_ready, o_ready, ont_ready = (
            sem("h_ready"), sem("q_ready"), sem("k_ready"), sem("probs_ready"), sem("o_ready"), sem("ont_ready"))
        v_ready, h2_hi_ready = sem("v_ready"), sem("h2_hi_ready")
        h2_ready, ex_ready, tanh_ready, actt_ready = (
            sem("h2_ready"), sem("ex_ready"), sem("tanh_ready"), sem("actt_ready"))
        eps1_step, rstd1_ready, eps2_step, rstd2_ready = (
            sem("eps1_step"), sem("rstd1_ready"), sem("eps2_step"), sem("rstd2_ready"))
        h2_lo_ready, wog_ready, actw_ready, out_ready = (
            sem("h2_lo_ready"), sem("wog_ready"), sem("actw_ready"), sem("out_ready"))

        def wait(eng, s, b, per, k):
            v = b * per + k
            if isinstance(v, int) and v <= 0:
                return
            eng.wait_ge(s, v)

        def steps(step):
            for i in range(B):
                step(i, i + 1 < B, i >= 1, i >= 2)

        ident = con[:, C_ID:C_ID + 128]

        def up_banks(b, t):
            return {(B - 2, 1): (0, 1), (B - 1, 0): (2, 3), (B - 1, 1): (0, 1)}.get((b, t), (W0, W1))

        def down_bank(b, t):
            return W1 if b < B - 1 else (OB, W2)[t]

        def value_block(source, g):
            dst = v_bd[g * KB:(g + 1) * KB, source:source + 1, 0:1, g * DH:g * DH + 1]
            src = ps[source * KB:(source + 1) * KB, OB, g * DH:g * DH + 1]
            return (view(dst, [[NSRC * NHG * VW, NT], [VW, NHG], [1, DH]]),
                    view(src, [[D, NT], [G * DH, NHG], [1, DH]]))

        block = ctx.enter_context(nc.Block())

        @block.sync
        def _(sp):
            def load_x(b):
                wait(sp, x1_ready, b - XBUF, 1, 1)
                sp.dma_start(x_sb[:, b % XBUF], x[b].rearrange("(t p) d -> p t d", p=128)).then_inc(x_loaded[b % XBUF], 16)

            def store(b, tiles):
                src = out_sb if b < B - 1 else out_last
                sp.dma_start(out[b].rearrange("(t p) d -> p t d", p=128)[:, tiles], src[:, tiles])\
                  .then_inc(out_stored, 16)

            def step(i, pre, tail, ffn):
                if i + 2 < B:
                    load_x(i + 2)
                if ffn:
                    wait(sp, out_ready, i - 2, 1, 1)
                    store(i - 2, slice(0, NT))

            load_x(0)
            sp.dma_start(wm_sb[:, 0:2 * D], wmod[:, 0:2 * D]).then_inc(mod1_loaded, 16)
            sp.dma_start(con[:], consts).then_inc(consts_loaded, 16)
            sp.dma_start(wqkv_sb[:], wqkv).then_inc(qkv_loaded, 16)
            sp.dma_start(wm_sb[:, 2 * D:], wmod[:, 2 * D:]).then_inc(mod_loaded, 16)
            load_x(1)
            for dst, src in ((wo_sb, wo), (gw_sb, gate_w), (bias_sb, bias), (wgu_sb, w_gu), (wd_sb, w_down)):
                sp.dma_start(dst[:], src).then_inc(w_loaded, 16)
            steps(step)
            sp.wait_ge(out_ready, B - 1)
            store(B - 2, slice(0, NT))
            for t in range(NT):
                sp.wait_ge(last_ready, t + 1)
                store(B - 1, slice(t, t + 1))
            sp.wait_ge(out_stored, 16 * (B - 1 + NT))

        @block.gpsimd
        def _(pool):
            def norm_scale(b, var, mv, veps, step_done, rs, used, ready):
                wait(pool, var, b, NT, NT)
                nc.gpsimd.tensor_scalar(veps[:], mv[:, :, 1], EPS, None, ALU.add).then_inc(step_done, 1)
                wait(pool, step_done, b, 1, 1)
                wait(pool, used, b, NT, 0)
                nc.gpsimd.tensor_tensor(rs[:], veps[:], minus_half[:], ALU.pow).then_inc(ready, 1)

            def scale_x(b):
                norm_scale(b, ln1_var, mv1, veps1, eps1_step, rstd1, xn1_ready, rstd1_ready)

            def scale_wo(i):
                pool.wait_ge(gate_row_ready, min(i // 2 + 1, 4))
                wait(pool, wo_ps, i, 1, 0)
                nc.gpsimd.tensor_tensor(wo_g[:], wo_sb[:], gate_row[:, i, 0, :], ALU.mult).then_inc(wog_ready, 1)

            def weigh_experts(b, t):
                wait(pool, cw_ready, b, 1, 1)
                wait(pool, act_ready, b, NT, t + 1)
                wait(pool, actt_ps, b, NT, 0)
                nc.gpsimd.tensor_tensor(
                    act_w[:, t, :].rearrange("p (e i) -> p e i", e=E),
                    act[:, t, :].rearrange("p (e i) -> p e i", e=E),
                    view(cw[:, t, :], [[1, E], [0, I]]), ALU.mult).then_inc(actw_ready, 1)

            def scale_x1(i):
                norm_scale(i, ln2_var, mv2, veps2, eps2_step, rstd2, xn2_ready, rstd2_ready)

            def low_part(i):
                wait(pool, h2_hi_ready, i, 1, 1)
                wait(pool, up_ps, i, NT, 0)
                nc.gpsimd.tensor_tensor(h2_lo[:], h2_t[:], h2_hi[:].bitcast(F32), ALU.subtract)\
                  .then_inc(h2_lo_ready, 1)

            def add_output(b):
                wait(pool, yg_ready, b, 1, 1)
                wait(pool, out_stored, b, 16, 0)
                nc.gpsimd.tensor_tensor(out_sb[:], y_g[:], x1[:, b % 2], ALU.add).then_inc(out_ready, 1)

            def step(i, pre, tail, ffn):
                if tail:
                    scale_wo(i - 1)
                if ffn:
                    weigh_experts(i - 2, 0)
                if tail:
                    scale_x1(i - 1)
                if pre and i > 0:
                    scale_x(i + 1)
                if ffn:
                    weigh_experts(i - 2, 1)
                if tail:
                    low_part(i - 1)
                if ffn:
                    add_output(i - 2)

            nc.gpsimd.memset(minus_half[:], -0.5).then_inc(zeroed, 1)
            nc.gpsimd.memset(q_pad[:], 0.0).then_inc(zeroed, 1)
            nc.gpsimd.memset(v_bd[:], 0.0).then_inc(zeroed, 1)
            nc.gpsimd.memset(o_t[:], 0.0).then_inc(zeroed, 1)
            pool.wait_ge(zeroed, 4)
            scale_x(0)
            scale_x(1)
            pool.wait_ge(w_loaded, 5 * 16)
            nc.gpsimd.tensor_copy(w_hi[:], wgu_sb[:]).then_inc(w_parts, 1)
            pool.wait_ge(w_parts, 1)
            nc.gpsimd.tensor_tensor(w_lo[:], wgu_sb[:], w_hi[:].bitcast(F32), ALU.subtract).then_inc(w_parts, 1)
            steps(step)
            scale_wo(B - 1)
            weigh_experts(B - 2, 0)
            scale_x1(B - 1)
            weigh_experts(B - 2, 1)
            low_part(B - 1)
            weigh_experts(B - 1, 0)
            weigh_experts(B - 1, 1)
            add_output(B - 2)

        @block.scalar
        def _(act_e):
            def modulate_x(b):
                wait(act_e, xt_ps, b, 1, 1)
                wait(act_e, v_ps, b, 1, 0)
                nc.scalar.activation(h_t[:], ps[:, W0, 0:S], ACT.Identity, scale=mod[:, CA, b:b + 1],
                                     bias=mod[:, SA, b:b + 1]).then_inc(h_ready, 1)

            def keep_q(b):
                wait(act_e, qk_ps, b, 1, 1)
                wait(act_e, scores_ps, b, PARTS, 0)
                for hg in range(NHG):
                    rows = slice(G * DH * hg, G * DH * (hg + 1))
                    last = nc.scalar.activation(q_pad[rows, hg, HALF:HALF + S], ps[rows, W0, 0:S], ACT.Copy)
                last.then_inc(q_ready, 1)

            def keep_v(b):
                wait(act_e, v_ps, b, 1, 1)
                wait(act_e, pv_ps, b, PARTS, 0)
                for source in range(NSRC):
                    for g in range(G):
                        dst, src = value_block(source, g)
                        last = nc.scalar.activation(dst, src, ACT.Copy)
                last.then_inc(v_ready, 1)

            def modulate_h2(i):
                wait(act_e, h2t_ps, i, 1, 1)
                wait(act_e, up_ps, i, NT, 0)
                nc.scalar.activation(h2_t[:], ps[:, W2, 0:S], ACT.Identity, scale=mod[:, CB, i:i + 1],
                                     bias=mod[:, SB, i:i + 1]).then_inc(h2_ready, 1)
                wait(act_e, h2_ready, i, 1, 1)
                nc.scalar.activation(h2_hi[:], h2_t[:], ACT.Copy).then_inc(h2_hi_ready, 1)

            def route_input(i):
                wait(act_e, logits_ps, i, 1, 1)
                wait(act_e, route_step, i, ROUTE, 0)
                nc.scalar.activation(ex[:].rearrange("p t e -> p (t e)"), ps[:, W2, 0:NT * E], ACT.Exp,
                                     scale=-1.0).then_inc(ex_ready, 1)

            def keep_gates(part):
                wait(act_e, gate_ps, part, 1, 1)
                nc.scalar.activation(gate_row[:, 2 * part:2 * part + 2].rearrange("p b w d -> p (b w d)"),
                                     ps[:, W2 if part == 1 else W1, :], ACT.Copy).then_inc(gate_row_ready, 1)

            def keep_on(i):
                wait(act_e, ont_ps, i, 1, 1)
                nc.scalar.activation(on_t[:], ps[:, W2, 0:S], ACT.Copy).then_inc(ont_ready, 1)

            def exponentials(i, pair, half):
                part = pair * HALVES + half + 1
                wait(act_e, shifted_ps, i, PARTS, part)
                wait(act_e, pv_ps, i - 1, PARTS, part)
                nc.scalar.activation(probs[:, pair, half * HB:(half + 1) * HB],
                                     ps[:, half * HB:(half + 1) * HB, 0:SC], ACT.Exp,
                                     scale=float(DH) ** -0.5).then_inc(probs_ready, 1)

            def keep_o(i):
                wait(act_e, pv_ps, i, PARTS, PARTS)
                wait(act_e, ot_ps, i, 1, 0)
                for p0 in (0, OP):
                    nc.scalar.activation(o_t[p0:p0 + VW].rearrange("p a q -> p (a q)"), ps[p0:p0 + VW, OB, :],
                                         ACT.Copy).then_inc(o_ready, 1)

            def tanh_gate(b, t):
                wait(act_e, up_ps, b, NT, t + 1)
                wait(act_e, gate_a_ready, b, NT, t)
                nc.scalar.activation(tanh_g[:], ps[:, up_banks(b, t)[0], :], ACT.Tanh, scale=0.5).then_inc(tanh_ready, 1)

            def keep_act_t(b, t):
                wait(act_e, actt_ps, b, NT, t + 1)
                nc.scalar.activation(act_t[:, t].rearrange("p c n -> p (c n)"), ps[:, W0 + t, :],
                                     ACT.Copy).then_inc(actt_ready, 1)

            def step(i, pre, tail, ffn):
                if tail:
                    keep_o(i - 1)
                if ffn:
                    tanh_gate(i - 2, 0)
                if tail:
                    keep_on(i - 1)
                if i < 2:
                    keep_gates(2 * i)
                exponentials(i, 0, 0)
                exponentials(i, 0, 1)
                if i < 2:
                    keep_gates(2 * i + 1)
                if i > 0:
                    keep_v(i)
                if ffn:
                    tanh_gate(i - 2, 1)
                if tail:
                    modulate_h2(i - 1)
                if i < 2:
                    modulate_x(i + 1)
                if ffn:
                    keep_act_t(i - 2, 0)
                    keep_act_t(i - 2, 1)
                if tail:
                    route_input(i - 1)
                exponentials(i, 1, 0)
                exponentials(i, 1, 1)
                if pre and i >= 2:
                    modulate_x(i + 1)
                if pre:
                    keep_q(i + 1)

            act_e.dma_start(ct_sb[:], c_t).then_inc(c_loaded, 16)
            nc.scalar.preload_act_table(ACT.Exp)
            act_e.wait_ge(c_loaded, 16)
            nc.scalar.activation(ct_t[:], ct_sb[:], ACT.Tanh, scale=0.5).then_inc(tanh_c_ready, 1)
            act_e.wait_ge(mod1_ready, 2)
            modulate_x(0)
            act_e.wait_ge(zeroed, 4)
            keep_q(0)
            keep_v(0)
            steps(step)
            keep_o(B - 1)
            tanh_gate(B - 2, 0)
            keep_on(B - 1)
            tanh_gate(B - 2, 1)
            keep_act_t(B - 2, 0)
            modulate_h2(B - 1)
            keep_act_t(B - 2, 1)
            route_input(B - 1)
            tanh_gate(B - 1, 0)
            tanh_gate(B - 1, 1)
            keep_act_t(B - 1, 0)
            keep_act_t(B - 1, 1)

        @block.tensor
        def _(pe):
            def transpose_norm(b, bank, xn, ready, done):
                wait(pe, ready, b, NT, NT)
                for t in range(NT):
                    last = nc.tensor.transpose(ps[:, bank, t * 128:(t + 1) * 128], xn[:, t, :], ident)
                last.then_inc(done, 1)

            def transpose_x(b):
                wait(pe, actt_ready, b - 3, NT, 1)
                transpose_norm(b, W0, xn1, xn1_ready, xt_ps)

            def project_qk(b):
                wait(pe, h_ready, b, 1, 1)
                nc.tensor.matmul(ps[:, W0, 0:S], wqkv_sb[:, 0], h_t[:], start=True, stop=True)
                if b == 1:
                    pe.wait_ge(gate_row_ready, 2)
                wait(pe, ex_ready, b - 2, 1, 1)
                nc.tensor.matmul(ps[:, W2, 0:S], wqkv_sb[:, 1], h_t[:], start=True, stop=True).then_inc(qk_ps, 1)

            def project_v(b):
                wait(pe, h_ready, b, 1, 1)
                wait(pe, o_ready, b - 1, 2, 2)
                for t in range(NT):
                    last = nc.tensor.matmul(ps[:, OB, t * D:(t + 1) * D], h_t[:, t * 128:(t + 1) * 128],
                                            wqkv_sb[:, 2], start=True, stop=True)
                last.then_inc(v_ps, 1)

            def scores(i, pair, half):
                if pair == 0 and half == 0:
                    wait(pe, k_ready, i, 1, 1)
                    wait(pe, q_ready, i, 1, 1)
                part = pair * HALVES + half + 1
                wait(pe, probs_ready, i, PARTS, part - HALVES)
                for kb in range(half * NKB // HALVES, (half + 1) * NKB // HALVES):
                    bank, j = kb // BANKKB, kb % BANKKB
                    nc.tensor.matmul(ps[:, bank, j * PAIR * WIN:(j + 1) * PAIR * WIN],
                                     k_bd[:, kb].rearrange("p g k -> p (g k)"),
                                     q_pad[:, pair * PAIR:(pair + 1) * PAIR, kb * KB:kb * KB + WIN],
                                     start=(j == 0), stop=False, skip_group_check=True)
                for bank in range(half * HB, (half + 1) * HB):
                    last = nc.tensor.matmul(
                        view(ps[:, bank, 0:1], [[WIN, BANKKB * PAIR], [2 * KB, 2], [1, KB]]), ident_bf[:],
                        view(mask_bf[:, 0, 0:1], [[0, BANKKB * PAIR], [KB, 2], [1, KB]]),
                        start=False, stop=False, skip_group_check=True)
                last.then_inc(scores_ps, 1)

            def subtract_max(i, pair):
                for half in range(HALVES):
                    wait(pe, shift_ready, i, PARTS, pair * HALVES + half + 1)
                    for bank in range(half * HB, (half + 1) * HB):
                        last = nc.tensor.matmul(
                            ps[:, bank, 0:SC], quad_ones[:],
                            view(shift[:, 0, bank * BANKKB * KB:bank * BANKKB * KB + 1],
                                 [[KB, BANKKB], [HALF + S + HALF, PAIR], [1, WIN]]),
                            start=False, stop=True, skip_group_check=True)
                    last.then_inc(shifted_ps, 1)

            def weigh_values(i, pair, half):
                wait(pe, probs_ready, i, PARTS, pair * HALVES + half + 1)
                if pair == 0 and half == 0:
                    wait(pe, v_ready, i, 1, 1)
                for kb in range(half * NKB // HALVES, (half + 1) * NKB // HALVES):
                    lo, hi = max(0, (kb - 1) * KB), min(S, (kb + 2) * KB)
                    for g in range(PAIR):
                        hg = pair * PAIR + g
                        p0, c0 = OP * g, S * pair
                        at = (kb % BANKKB * PAIR + g) * WIN + lo - (kb - 1) * KB
                        last = nc.tensor.matmul(ps[p0:p0 + VW, OB, c0 + lo:c0 + hi],
                                                v_bd[:, kb, hg, :], probs[:, pair, kb // BANKKB, at:at + hi - lo],
                                                start=(pair == 0 and kb == 0), stop=(kb == NKB - 1),
                                                skip_group_check=True)
                last.then_inc(pv_ps, 1)

            def logits(b):
                if b == 0:
                    pe.wait_ge(w_loaded, 5 * 16)
                wait(pe, h2_ready, b, 1, 1)
                for t in range(NT):
                    last = nc.tensor.matmul(ps[:, W2, t * E:(t + 1) * E], h2_t[:, t * 128:(t + 1) * 128],
                                            gw_sb[:], start=True, stop=True)
                last.then_inc(logits_ps, 1)

            def up(b, t):
                if t == 0:
                    if b + 2 < B:
                        wait(pe, q_ready, b + 2, 1, 1)
                    if b == 0:
                        pe.wait_ge(w_parts, 2)
                        pe.wait_ge(gate_row_ready, 4)
                    wait(pe, h2_hi_ready, b, 1, 1)
                    wait(pe, h2_lo_ready, b, 1, 1)
                    if b < B - 1:
                        wait(pe, yg_ready, b - 1, 1, 1)
                    else:
                        wait(pe, probs_ready, b, PARTS, PARTS)
                elif b < B - 2:
                    wait(pe, act_ready, b, NT, t)
                elif b == B - 2:
                    wait(pe, probs_ready, B - 1, PARTS, PARTS - 1)
                else:
                    wait(pe, act_ready, B - 2, NT, NT)
                tok = slice(t * 128, (t + 1) * 128)
                for w in range(2):
                    bank = up_banks(b, t)[w]
                    nc.tensor.matmul(ps[:, bank, :], h2_hi[:, tok], w_hi[:, w], start=True, stop=False)
                    nc.tensor.matmul(ps[:, bank, :], h2_hi[:, tok], w_lo[:, w], start=False, stop=False)
                    last = nc.tensor.matmul(ps[:, bank, :], h2_lo[:, tok], w_hi[:, w], start=False, stop=True)
                last.then_inc(up_ps, 1)

            def transpose_act(b, t):
                wait(pe, actw_ready, b, NT, t + 1)
                if b < B - 1:
                    wait(pe, act_ready, b, NT, NT if b < B - 2 else 1)
                elif t == 1:
                    wait(pe, yg_ready, b - 1, 1, 1)
                for c in range(NC_):
                    last = nc.tensor.transpose(ps[:, W0 + t, c * 128:(c + 1) * 128],
                                               act_w[:, t, c * 128:(c + 1) * 128], ident)
                last.then_inc(actt_ps, 1)

            def down(b, t):
                wait(pe, actt_ready, b, NT, NT if b < B - 1 else t + 1)
                for c in range(NC_):
                    last = nc.tensor.matmul(ps[:, down_bank(b, t), t * D:(t + 1) * D], act_t[:, t, c, :],
                                            wd_sb[:, c, :], start=(c == 0), stop=(c == NC_ - 1))
                last.then_inc(down_ps, 1)

            def transpose_o(i):
                wait(pe, o_ready, i, 2, 2)
                wait(pe, ex_ready, i - 1, 1, 1)
                if i + 1 < B:
                    wait(pe, k_ready, i + 1, 1, 1)
                for t in range(NT):
                    for pair in range(2):
                        at = (t * 2 + pair) * 128
                        last = nc.tensor.transpose(ps[:, W2, at:at + OP + VW], o_t[:, pair, t * 128:(t + 1) * 128],
                                                   con[0:OP + VW, C_ID:C_ID + OP + VW])
                last.then_inc(ot_ps, 1)

            def transpose_on(i):
                wait(pe, on_ready, i, 1, 1)
                for t in range(NT):
                    last = nc.tensor.transpose(ps[:, W2, t * 128:(t + 1) * 128], o_n[:, t, :], ident)
                last.then_inc(ont_ps, 1)

            def output_projection(i):
                wait(pe, ont_ready, i, 1, 1)
                wait(pe, wog_ready, i, 1, 1)
                for t in range(NT):
                    last = nc.tensor.matmul(ps[:, W2, t * D:(t + 1) * D], on_t[:, t * 128:(t + 1) * 128],
                                            wo_g[:], start=True, stop=True)
                last.then_inc(wo_ps, 1)

            def transpose_x1(i):
                wait(pe, x1_ready, i, 1, 1)
                transpose_norm(i, W2, xn2, xn2_ready, h2t_ps)

            def modulation(js, bank):
                for j in js:
                    last = nc.tensor.matmul(ps[:, bank, j * B:(j + 1) * B], wm_sb[:, j * D:(j + 1) * D], silu_c[:],
                                            start=True, stop=True)
                last.then_inc(mod_ps, 1)

            def gates_part(part):
                if part == 0:
                    pe.wait_ge(mod_step, 6)
                if part >= 2:
                    pe.wait_ge(gate_row_ready, 1 if part == 2 else 3)
                for n in range(4):
                    last = nc.tensor.matmul(ps[:, W2 if part == 1 else W1, n * D:(n + 1) * D],
                                            view(gates[:, n % 2, 2 * part + n // 2:2 * part + n // 2 + 1], [[0, 128]]),
                                            ident, start=True, stop=True)
                last.then_inc(gate_ps, 1)

            def step(i, pre, tail, ffn):
                scores(i, 0, 0)
                if i == 0:
                    pe.wait_ge(mod_loaded, 16)
                    modulation((GA, SB, CB, GB), W2)
                if tail:
                    transpose_o(i - 1)
                scores(i, 0, 1)
                if i > 0:
                    project_v(i)
                if ffn:
                    up(i - 2, 0)
                if tail:
                    transpose_on(i - 1)
                if i < 2:
                    gates_part(2 * i)
                subtract_max(i, 0)
                if i < 2:
                    gates_part(2 * i + 1)
                if tail:
                    output_projection(i - 1)
                scores(i, 1, 0)
                if ffn:
                    up(i - 2, 1)
                weigh_values(i, 0, 0)
                scores(i, 1, 1)
                weigh_values(i, 0, 1)
                if tail:
                    transpose_x1(i - 1)
                if i < 2:
                    transpose_x(i + 1)
                if ffn:
                    transpose_act(i - 2, 0)
                    transpose_act(i - 2, 1)
                if tail:
                    logits(i - 1)
                subtract_max(i, 1)
                if pre and i >= 2:
                    transpose_x(i + 1)
                if ffn:
                    down(i - 2, 0)
                    down(i - 2, 1)
                if pre:
                    project_qk(i + 1)
                weigh_values(i, 1, 0)
                weigh_values(i, 1, 1)

            pe.wait_ge(silu_step, 2)
            pe.wait_ge(mod1_loaded, 16)
            modulation((SA, CA), W1)
            pe.wait_ge(consts_loaded, 16)
            transpose_x(0)
            pe.wait_ge(qkv_loaded, 16)
            project_qk(0)
            project_v(0)
            pe.wait_ge(consts_made, 5)
            pe.wait_ge(dens_made, 1)
            steps(step)
            up(B - 2, 0)
            transpose_o(B - 1)
            up(B - 2, 1)
            transpose_on(B - 1)
            output_projection(B - 1)
            transpose_act(B - 2, 0)
            transpose_x1(B - 1)
            transpose_act(B - 2, 1)
            logits(B - 1)
            down(B - 2, 0)
            up(B - 1, 0)
            up(B - 1, 1)
            down(B - 2, 1)
            for t in range(NT):
                transpose_act(B - 1, t)
            for t in range(NT):
                down(B - 1, t)

        @block.vector
        def _(dve):
            def norm_stats(b, xs, stats, stat, mv, var):
                for t in range(NT):
                    nc.vector.bn_stats(stats[:, t, :], xs[:, t, :]).then_inc(stat, 1)
                wait(dve, stat, b, NT, NT)
                for t in range(NT):
                    nc.vector.bn_aggr(mv[:, t, :], stats[:, t, :]).then_inc(var, 1)

            def normalise(b, xs, mv, rs, rs_ready, xn, ready):
                wait(dve, rs_ready, b, 1, 1)
                for t in range(NT):
                    nc.vector.tensor_scalar(xn[:, t, :], xs[:, t, :], mv[:, t, 0:1], rs[:, t:t + 1],
                                            ALU.subtract, ALU.mult).then_inc(ready, 1)

            def norm1(b):
                wait(dve, x_loaded[b % XBUF], b // XBUF, 16, 16)
                norm_stats(b, x_sb[:, b % XBUF], stats1, ln1_stat, mv1, ln1_var)

            def norm1_apply(b):
                wait(dve, xt_ps, b, 1, 0)
                normalise(b, x_sb[:, b % XBUF], mv1, rstd1, rstd1_ready, xn1, xn1_ready)

            def keep_k(b):
                wait(dve, qk_ps, b, 1, 1)
                wait(dve, scores_ps, b, PARTS, 0)
                nc.vector.tensor_tensor(k_bd[:], view(ps[:, W2, 0:1], [[KB, NKB], [0, G], [1, KB]]),
                                        view(con[:, C_HEAD:C_HEAD + 1], [[0, NKB], [1, G], [0, KB]]),
                                        ALU.mult).then_inc(k_ready, 1)

            def block_max(i, pair, half):
                wait(dve, scores_ps, i, PARTS, pair * HALVES + half + 1)
                wait(dve, rowmax_ready, i, NPAIR, pair)
                n = 3 * PAIR * NKB // HALVES
                nc.vector.tensor_reduce(
                    blkmax[:, PAD + half * n:PAD + (half + 1) * n],
                    view(ps[:, half * HB, 0:1], [[BANK, HB], [KB, SC // KB], [1, KB]]),
                    AX.X, ALU.max, apply_transpose=True).then_inc(blkmax_ready, 1)

            def row_maximum(i, pair):
                wait(dve, blkmax_ready, i, PARTS, (pair + 1) * HALVES)
                wait(dve, shift_ready, i, PARTS, pair * HALVES)
                nc.vector.tensor_reduce(
                    row_max[:], view(blkmax[:, PAD + 2 - 3 * PAIR:PAD + 3 - 3 * PAIR],
                                     [[3 * PAIR, NKB], [3, PAIR], [3 * PAIR - 1, 3]]),
                    AX.X, ALU.max).then_inc(rowmax_ready, 1)
                wait(dve, rowmax_ready, i, NPAIR, pair + 1)
                wait(dve, shifted_ps, i, PARTS, pair * HALVES)
                for q0, q1 in ((0, NKB // HALVES + 1), (NKB // HALVES + 1, NKB)):
                    at = HALF + q0 * KB
                    nc.vector.tensor_tensor(
                        view(shift[:, 0, at:at + 1], [[HALF + S + HALF, PAIR], [KB, q1 - q0], [1, KB]]),
                        view(row_max[:, q0, 0:1], [[1, PAIR], [PAIR, q1 - q0], [0, KB]]),
                        view(con[:, C_NI:C_NI + 1], [[0, PAIR], [0, q1 - q0], [1, KB]]), ALU.mult)\
                      .then_inc(shift_ready, 1)

            def route_chain(b, start):
                n = [start]

                def then(ins):
                    n[0] += 1
                    ins.then_inc(route_step, 1)
                    wait(dve, route_step, b, ROUTE, n[0])

                def compare(dst_gt, dst_eq, v, count):
                    mine = view(v[:], [[count, NT], [1, count], [0, count]])
                    other = view(v[:], [[count, NT], [0, count], [1, count]])
                    nc.vector.tensor_tensor(dst_gt[:], other, mine, ALU.is_gt).then_inc(rank_gt, 1)
                    then(nc.vector.tensor_tensor(dst_eq[:], other, mine, ALU.is_equal))

                def before(dst_gt, dst_eq, dst_tie, dst_all, dst_rank, count, tie):
                    then(nc.vector.tensor_tensor(
                        dst_tie[:].rearrange("p t a b -> p t (a b)"), dst_eq[:].rearrange("p t a b -> p t (a b)"),
                        view(con[:, tie:tie + 1], [[0, NT], [1, count * count]]), ALU.mult))
                    dve.wait_ge(rank_gt, b * 2 + (1 if count == NG else 2))
                    then(nc.vector.tensor_tensor(dst_all[:], dst_gt[:], dst_tie[:], ALU.add))
                    then(nc.vector.tensor_reduce(dst_rank[:].rearrange("p t a -> p (t a)"),
                                                 dst_all[:].rearrange("p t a b -> p (t a) b"), AX.X, ALU.add))

                return n, then, compare, before

            def route_compare(b):
                wait(dve, ex_ready, b, 1, 1)
                n, then, compare, before = route_chain(b, 0)
                then(nc.vector.tensor_scalar(exp1[:], ex[:], 1.0, None, ALU.add))
                then(nc.vector.reciprocal(score[:], exp1[:]))
                then(nc.vector.tensor_tensor(choice[:], score[:], bias_sb[:], ALU.add))
                then(nc.vector.tensor_tensor(gsum[:], choice[:, :, 0::2], choice[:, :, 1::2], ALU.add))
                compare(ggt, geq, gsum, NG)
                before(ggt, geq, gtie, gall, grank, NG, C_LG)
                then(nc.vector.scalar_tensor_tensor(
                    out=tmp[:].rearrange("p t (g e) -> p (t g) e", e=GSZ),
                    in0=view(grank[:], [[1, NT * NG], [0, GSZ]]), scalar=TOPKG - 0.5,
                    in1=choice[:].rearrange("p t (g e) -> p (t g) e", e=GSZ), op0=ALU.is_lt, op1=ALU.mult))
                compare(egt, eeq, tmp, E)
                assert n[0] == COMPARE_STEPS

            def route_weights(b):
                wait(dve, actw_ready, b, NT, 0)
                n, then, _, before = route_chain(b, COMPARE_STEPS)
                before(egt, eeq, etie, eall, rank, E, C_LE)
                flat = "p t e -> p (t e)"
                then(nc.vector.scalar_tensor_tensor(
                    out=wsel[:].rearrange(flat), in0=rank[:].rearrange(flat), scalar=TOPK - 0.5,
                    in1=score[:].rearrange(flat), op0=ALU.is_lt, op1=ALU.mult))
                then(nc.vector.tensor_reduce(wsum[:], wsel[:], AX.X, ALU.add))
                then(nc.vector.tensor_scalar(wsum2[:], wsum[:], 1e-20, 2.0, ALU.add, ALU.mult))
                then(nc.vector.reciprocal(rsum[:], wsum2[:]))
                nc.vector.tensor_tensor(cw[:], wsel[:], view(rsum[:], [[1, NT], [0, E]]), ALU.mult)\
                  .then_inc(cw_ready, 1)
                assert n[0] == ROUTE

            def activate(b, t):
                wait(dve, tanh_ready, b, NT, t + 1)
                wait(dve, act_ready, b, NT, t)
                nc.vector.scalar_tensor_tensor(out=gate_a[:], in0=tanh_g[:], scalar=1.0, in1=ps[:, up_banks(b, t)[0], :],
                                               op0=ALU.add, op1=ALU.mult).then_inc(gate_a_ready, 1)
                wait(dve, gate_a_ready, b, NT, t + 1)
                wait(dve, actw_ready, b, NT, 0)
                nc.vector.tensor_tensor(act[:, t, :], gate_a[:], ps[:, up_banks(b, t)[1], :], ALU.mult).then_inc(act_ready, 1)

            def normalise_o(i):
                wait(dve, ot_ps, i, 1, 1)
                nc.vector.reciprocal(
                    rden[:].rearrange("p t (a g) -> p (t a) g", g=G),
                    view(ps[:, W2, G * DH:G * DH + 1], [[OP, NT * NHG], [1, G]])).then_inc(rden_ready, 1)
                wait(dve, rden_ready, i, 1, 1)
                nc.vector.tensor_tensor(
                    o_n[:].rearrange("p t (a g d) -> p (t a) g d", a=NHG, g=G),
                    view(ps[:, W2, 0:1], [[OP, NT * NHG], [DH, G], [1, DH]]),
                    view(rden[:, 0, 0:1], [[G, NT * NHG], [1, G], [0, DH]]), ALU.mult).then_inc(on_ready, 1)

            def residual(i):
                wait(dve, wo_ps, i, 1, 1)
                wait(dve, out_ready, i - 2, 1, 1)
                nc.vector.tensor_tensor(x1[:, i % 2], ps[:, W2, 0:NT * D].rearrange("p (t d) -> p t d", t=NT),
                                        x_sb[:, i % XBUF], ALU.add).then_inc(x1_ready, 1)
                wait(dve, x1_ready, i, 1, 1)
                norm_stats(i, x1[:, i % 2], stats2, ln2_stat, mv2, ln2_var)

            def gate_output(b):
                wait(dve, down_ps, b, NT, NT)
                wait(dve, out_ready, b, 1, 0)
                nc.vector.tensor_tensor(
                    y_g[:], ps[:, W1, 0:NT * D].rearrange("p (t d) -> p t d", t=NT),
                    view(gate_row[:, b, 1, :], [[0, NT], [1, D]]), ALU.mult).then_inc(yg_ready, 1)

            def finish_output(t):
                b = B - 1
                wait(dve, down_ps, b, NT, t + 1)
                nc.vector.tensor_tensor(y_last[:, t], ps[:, down_bank(b, t), t * D:(t + 1) * D],
                                        gate_row[:, b, 1, :], ALU.mult).then_inc(yg_ready, 1)
                dve.wait_ge(yg_ready, B + t)
                nc.vector.tensor_tensor(out_last[:, t], y_last[:, t], x1[:, b % 2, t], ALU.add)\
                  .then_inc(last_ready, 1)

            def apply_norm2(i):
                wait(dve, h2t_ps, i, 1, 0)
                normalise(i, x1[:, i % 2], mv2, rstd2, rstd2_ready, xn2, xn2_ready)

            def finish_modulation():
                dve.wait_ge(mod_ps, 2)
                nc.vector.tensor_copy(mod[:, GA:].rearrange("p m b -> p (m b)"), ps[:, W2, GA * B:MODS * B])\
                  .then_inc(mod_step, 1)
                dve.wait_ge(mod_step, 1)
                nc.vector.tensor_scalar(mod[:, CB, :], mod[:, CB, :], 1.0, None, ALU.add).then_inc(mod_step, 1)
                nc.vector.tensor_scalar(gsign[:], mod[:, GA::3, :], 0.0, 2.0, ALU.is_ge, ALU.mult).then_inc(mod_step, 1)
                nc.vector.scalar_tensor_tensor(out=gabs[:], in0=mod[:, GA::3, :], scalar=-1.0, in1=mod[:, GA::3, :],
                                               op0=ALU.mult, op1=ALU.max).then_inc(mod_step, 1)
                dve.wait_ge(mod_step, 4)
                nc.vector.tensor_scalar(gsize[:], gabs[:], GATE_MIN, None, ALU.max).then_inc(mod_step, 1)
                dve.wait_ge(mod_step, 5)
                nc.vector.scalar_tensor_tensor(out=gates[:], in0=gsign[:], scalar=-1.0, in1=gsize[:],
                                               op0=ALU.add, op1=ALU.mult).then_inc(mod_step, 1)

            def step(i, pre, tail, ffn):
                block_max(i, 0, 0)
                if i == 0:
                    finish_modulation()
                if tail:
                    normalise_o(i - 1)
                block_max(i, 0, 1)
                row_maximum(i, 0)
                if ffn:
                    activate(i - 2, 0)
                if tail:
                    residual(i - 1)
                if pre and i > 0:
                    norm1(i + 1)
                block_max(i, 1, 0)
                if tail:
                    apply_norm2(i - 1)
                if ffn:
                    activate(i - 2, 1)
                if pre and i > 0:
                    norm1_apply(i + 1)
                block_max(i, 1, 1)
                row_maximum(i, 1)
                if tail:
                    route_compare(i - 1)
                if pre:
                    keep_k(i + 1)
                if ffn:
                    gate_output(i - 2)
                if tail:
                    route_weights(i - 1)

            dve.memset(blkmax[:], -3e38).then_inc(consts_made, 1)
            dve.memset(shift[:].bitcast(F32), 0.0).then_inc(consts_made, 1)
            norm1(0)
            dve.wait_ge(tanh_c_ready, 1)
            nc.vector.scalar_tensor_tensor(out=silu2_c[:], in0=ct_t[:], scalar=1.0, in1=ct_sb[:],
                                           op0=ALU.add, op1=ALU.mult).then_inc(silu_step, 1)
            dve.wait_ge(silu_step, 1)
            nc.vector.tensor_scalar(silu_c[:], silu2_c[:], 0.5, None, ALU.mult).then_inc(silu_step, 1)
            norm1_apply(0)
            dve.wait_ge(mod_ps, 1)
            nc.vector.tensor_copy(mod[:, SA, :], ps[:, W1, SA * B:(SA + 1) * B]).then_inc(mod1_ready, 1)
            nc.vector.tensor_scalar(mod[:, CA, :], ps[:, W1, CA * B:(CA + 1) * B], 1.0, None, ALU.add)\
              .then_inc(mod1_ready, 1)
            dve.wait_ge(consts_loaded, 16)
            nc.vector.tensor_copy(ident_bf[:], ident).then_inc(consts_made, 1)
            nc.vector.tensor_copy(mask_bf[:].rearrange("p a q -> p (a q)"),
                                  con[:, C_MASK:C_MASK + 2 * KB]).then_inc(consts_made, 1)
            nc.vector.tensor_copy(quad_ones[:], con[:, C_ONES:C_ONES + 128]).then_inc(consts_made, 1)
            dve.wait_ge(zeroed, 4)
            nc.vector.tensor_copy(view(v_bd[:, 0, 0, G * DH:G * DH + 1], [[VW, NKB * NHG], [1, G]]),
                                  view(con[:, C_DEN:C_DEN + 1], [[0, NKB * NHG], [1, G]])).then_inc(dens_made, 1)
            keep_k(0)
            norm1(1)
            norm1_apply(1)
            steps(step)
            normalise_o(B - 1)
            activate(B - 2, 0)
            residual(B - 1)
            activate(B - 2, 1)
            apply_norm2(B - 1)
            route_compare(B - 1)
            route_weights(B - 1)
            activate(B - 1, 0)
            activate(B - 1, 1)
            gate_output(B - 2)
            for t in range(NT):
                finish_output(t)


def launch_inputs(a):
    t = np.ascontiguousarray
    wqkv = a["L0_attn_W_qkv"]
    up = lambda w: t(w.reshape(EI, D).T)
    return {
        "x": t(a["L0_attn_x"]),
        "wqkv": t(wqkv.reshape(3, D, D).transpose(2, 0, 1)),
        "wo": t(a["L0_attn_W_o"].T),
        "gate_w": t(a["L0_ffn_gate_weight"].T),
        "bias": t(np.broadcast_to(a["L0_ffn_e_score_correction_bias"], (128, NT, E))),
        "w_gu": t(np.stack([up(a["L0_ffn_gate_proj"]), up(a["L0_ffn_up_proj"])], axis=1)),
        "w_down": t(a["L0_ffn_down_proj"].transpose(0, 2, 1).reshape(NC_, 128, D).transpose(1, 0, 2)),
        "c_t": t(a["L0_c"].T), "wmod": t(a["L0_wmod"]),
        "consts": constants(),
    }


def kernel(**inputs):
    import concourse.bacc as bacc
    from concourse.bass_utils import run_bass_kernel_spmd

    nc = bacc.Bacc("TRN2", target_bir_lowering=False, num_devices=1)
    arrays = launch_inputs({k: np.asarray(v) for k, v in inputs.items()})
    aps = {k: nc.dram_tensor(k, v.shape, F32, kind="ExternalInput").ap() for k, v in arrays.items()}
    out = nc.dram_tensor("out", (B, S, D), F32, kind="ExternalOutput").ap()
    program(nc, out=out, **aps)
    return run_bass_kernel_spmd(nc, [arrays], core_ids=[0]).results[0]["out"]
```
